# Optimizing a Trainium2 kernel written in Bass

```python
import numpy as np
import jax
import jax.numpy as jnp

def _softmax(x, axis=-1):
    return jax.nn.softmax(x, axis=axis)
def _gelu(x):
    return jax.nn.gelu(x, approximate=True)
def _silu(x):
    return jax.nn.silu(x)
def _sigmoid(x):
    return jax.nn.sigmoid(x)
def _layernorm(x, axis=-1, eps=1e-5):
    m = jnp.mean(x, axis=axis, keepdims=True)
    v = jnp.var(x, axis=axis, keepdims=True)
    return (x - m) / jnp.sqrt(v + eps)
def _scatter_add(tgt, idx, src, axis=0):
    return tgt.at[idx].add(src)
def _segment_sum(src, seg, n):
    return jax.ops.segment_sum(src, seg, n)

kernel_name = 'mk_adj_resnorm_d2_adj_128_af715c'

def setup_inputs(seed: int = 0):
    np.random.seed(seed)
    _w = jnp.asarray
    def _rec_inputs():
        import jax
        import jax.numpy as jnp
        _gk = jax.random.key(seed)
        x = -0.0005207 + 1.001 * jax.random.normal(jax.random.fold_in(_gk, 1), (8, 2048, 128), jnp.float32)
        _a = jax.random.bernoulli(jax.random.fold_in(_gk, 2), 0.00390625, (8, 2048, 2048))
        _a = jnp.logical_or(_a, jnp.swapaxes(_a, -1, -2))
        _a = jnp.logical_or(_a, jnp.eye(2048, dtype=bool))
        _af = _a.astype(jnp.float32)
        _af = _af * jax.random.uniform(jax.random.fold_in(_gk, 3), (8, 2048, 2048), jnp.float32, 0.05, 1)
        adj = _af
        _nm = jnp.ones((8, 2048), dtype=bool)
        nodemask = jnp.where(_nm, 1.0, 0.0).astype(jnp.int32)
        return x, adj, nodemask
    x, adj, nodemask = _rec_inputs()
    def _L0_gnn_setup():
        import jax, jax.numpy as jnp
        import numpy as np
        EPS = 1e-06

        def _normalize(A):
            n = A.shape[-1]
            eye = jnp.eye(n, dtype=A.dtype)
            A_hat = A * (1.0 - eye) + eye
            d = 1.0 / (EPS + jnp.sqrt(jnp.sum(A_hat, axis=2)))
            return A_hat * d[:, :, None] * d[:, None, :]
        key = jax.random.key(seed)
        k1, k2, k3 = jax.random.split(key, 3)
        B, N, F, O = (8, 2048, 128, 128)
        x = jax.random.normal(k1, (B, N, F), dtype=jnp.float32)
        adj = jax.random.uniform(k2, (B, N, N), dtype=jnp.float32)
        kernel = jax.random.normal(k3, (F, O), dtype=jnp.float32) * 0.05
        return {'x': x, 'adj': adj, 'kernel': kernel}
    _L0_gnn_all = _L0_gnn_setup()
    _L0_gnn_in = {k: v for k, v in _L0_gnn_all.items() if k in ('kernel', )}
    del _L0_gnn_all

    def _L1_gnn_setup():
        import jax, jax.numpy as jnp
        import numpy as np
        T_DIL = 10
        K_DIL = 2
        BN_EPS = 1e-05
        NORM_EPS = 1e-12

        def _dilate_pattern(adj_bool, mask_b):
            N = adj_bool.shape[0]

            def step(carry, n):
                row = jnp.take(carry, n, axis=0)
                nbi = row.astype(jnp.int32)
                num = jnp.sum(nbi)
                sf = jnp.where(num > T_DIL, (num + K_DIL - 1) // K_DIL, 1)
                rank = jnp.cumsum(nbi)
                rm = row & (rank % sf == 0)
                valid = (mask_b[n] != 0) & (num > 1)
                rm = jnp.where(valid, rm, False)
                keep = ~rm
                carry = carry.at[n].set(row & keep)
                carry = carry.at[:, n].set(carry[:, n] & keep)
                return (carry, None)
            out, _ = jax.lax.scan(step, adj_bool, jnp.arange(N))
            return out

        def _dilate(adj, mask):
            keep = jax.vmap(_dilate_pattern)(adj > 0, mask)
            return adj * keep.astype(adj.dtype)

        def _sage(x, adj, Wr, Wx, b, mf):
            deg = jnp.clip(jnp.sum(adj, axis=-1, keepdims=True), 1.0, None)
            agg = jnp.einsum('bij,bjd->bid', adj, x) / deg
            out = agg @ Wr + x @ Wx + b
            nrm = jnp.maximum(jnp.linalg.norm(out, axis=-1, keepdims=True), NORM_EPS)
            return out / nrm * mf[..., None]

        def _bn(x, g, b):
            m = jnp.mean(x, axis=(0, 1))
            v = jnp.var(x, axis=(0, 1))
            return (x - m) * jax.lax.rsqrt(v + BN_EPS) * g + b

        def _forward(x, adj, mask, Wr1, Wx1, b1, g1, be1, Wr2, Wx2, b2, g2, be2, Wr3, Wx3, b3, g3, be3, Wl, bl):
            mf = mask.astype(x.dtype)
            adj_d = _dilate(adj, mask)
            h1 = _bn(jax.nn.relu(_sage(x, adj_d, Wr1, Wx1, b1, mf)), g1, be1)
            h2 = _bn(jax.nn.relu(_sage(h1, adj_d, Wr2, Wx2, b2, mf)), g2, be2)
            h3 = _bn(jax.nn.relu(_sage(h2, adj_d, Wr3, Wx3, b3, mf)), g3, be3)
            xc = jnp.concatenate([h1, h2, h3], axis=-1) * mf[..., None]
            return (xc @ Wl + bl) * mf[..., None]
        B, N, D, H, E = (8, 2048, 128, 128, 128)
        key = jax.random.key(seed)
        ks = jax.random.split(key, 24)
        x = jax.random.normal(ks[0], (B, N, D), dtype=jnp.float32)
        a = jax.random.bernoulli(ks[1], 0.01, (B, N, N))
        a = a | jnp.swapaxes(a, 1, 2)
        a = a & ~jnp.eye(N, dtype=bool)[None]
        adj = a.astype(jnp.float32)
        mask = jnp.ones((B, N), dtype=jnp.int32)
        s = 0.05
        p = {}
        dims = [(D, H), (H, H), (H, E)]
        for i, (di, do) in enumerate(dims, 1):
            p[f'Wr{i}'] = s * jax.random.normal(ks[2 * i], (di, do), dtype=jnp.float32)
            p[f'Wx{i}'] = s * jax.random.normal(ks[2 * i + 1], (di, do), dtype=jnp.float32)
            p[f'b{i}'] = jnp.zeros((do,), dtype=jnp.float32)
            p[f'g{i}'] = jnp.ones((do,), dtype=jnp.float32)
            p[f'be{i}'] = jnp.zeros((do,), dtype=jnp.float32)
        p['Wl'] = s * jax.random.normal(ks[10], (2 * H + E, E), dtype=jnp.float32)
        p['bl'] = jnp.zeros((E,), dtype=jnp.float32)
        return {'x': x, 'adj': adj, 'mask': mask, **p}
    _L1_gnn_all = _L1_gnn_setup()
    _L1_gnn_in = {k: v for k, v in _L1_gnn_all.items() if k in ('Wr1', 'Wx1', 'b1', 'g1', 'be1', 'Wr2', 'Wx2', 'b2', 'g2', 'be2', 'Wr3', 'Wx3', 'b3', 'g3', 'be3', 'Wl', 'bl', )}
    del _L1_gnn_all

    return {
        "x": x,
        "adj": adj,
        "nodemask": nodemask,
        "L0_gnn_kernel": _L0_gnn_in["kernel"],
        "L1_gnn_Wr1": _L1_gnn_in["Wr1"],
        "L1_gnn_Wx1": _L1_gnn_in["Wx1"],
        "L1_gnn_b1": _L1_gnn_in["b1"],
        "L1_gnn_g1": _L1_gnn_in["g1"],
        "L1_gnn_be1": _L1_gnn_in["be1"],
        "L1_gnn_Wr2": _L1_gnn_in["Wr2"],
        "L1_gnn_Wx2": _L1_gnn_in["Wx2"],
        "L1_gnn_b2": _L1_gnn_in["b2"],
        "L1_gnn_g2": _L1_gnn_in["g2"],
        "L1_gnn_be2": _L1_gnn_in["be2"],
        "L1_gnn_Wr3": _L1_gnn_in["Wr3"],
        "L1_gnn_Wx3": _L1_gnn_in["Wx3"],
        "L1_gnn_b3": _L1_gnn_in["b3"],
        "L1_gnn_g3": _L1_gnn_in["g3"],
        "L1_gnn_be3": _L1_gnn_in["be3"],
        "L1_gnn_Wl": _L1_gnn_in["Wl"],
        "L1_gnn_bl": _L1_gnn_in["bl"],
    }

def reference(x, adj, nodemask, L0_gnn_kernel, L1_gnn_Wr1, L1_gnn_Wx1, L1_gnn_b1, L1_gnn_g1, L1_gnn_be1, L1_gnn_Wr2, L1_gnn_Wx2, L1_gnn_b2, L1_gnn_g2, L1_gnn_be2, L1_gnn_Wr3, L1_gnn_Wx3, L1_gnn_b3, L1_gnn_g3, L1_gnn_be3, L1_gnn_Wl, L1_gnn_bl):
    import jax
    import jax.numpy as jnp
    def _L0_gnn_ref(x, adj, kernel):
        import jax, jax.numpy as jnp
        import numpy as np
        EPS = 1e-06

        def _normalize(A):
            n = A.shape[-1]
            eye = jnp.eye(n, dtype=A.dtype)
            A_hat = A * (1.0 - eye) + eye
            d = 1.0 / (EPS + jnp.sqrt(jnp.sum(A_hat, axis=2)))
            return A_hat * d[:, :, None] * d[:, None, :]
        norm = _normalize(adj)
        agg = jnp.einsum('bnm,bmf->bnf', norm, x)
        out = jnp.einsum('bnf,fo->bno', agg, kernel)
        return jax.nn.relu(out)

    def _L1_gnn_ref(x, adj, mask, Wr1, Wx1, b1, g1, be1, Wr2, Wx2, b2, g2, be2, Wr3, Wx3, b3, g3, be3, Wl, bl):
        import jax, jax.numpy as jnp
        import numpy as np
        T_DIL = 10
        K_DIL = 2
        BN_EPS = 1e-05
        NORM_EPS = 1e-12

        def _dilate_pattern(adj_bool, mask_b):
            N = adj_bool.shape[0]

            def step(carry, n):
                row = jnp.take(carry, n, axis=0)
                nbi = row.astype(jnp.int32)
                num = jnp.sum(nbi)
                sf = jnp.where(num > T_DIL, (num + K_DIL - 1) // K_DIL, 1)
                rank = jnp.cumsum(nbi)
                rm = row & (rank % sf == 0)
                valid = (mask_b[n] != 0) & (num > 1)
                rm = jnp.where(valid, rm, False)
                keep = ~rm
                carry = carry.at[n].set(row & keep)
                carry = carry.at[:, n].set(carry[:, n] & keep)
                return (carry, None)
            out, _ = jax.lax.scan(step, adj_bool, jnp.arange(N))
            return out

        def _dilate(adj, mask):
            keep = jax.vmap(_dilate_pattern)(adj > 0, mask)
            return adj * keep.astype(adj.dtype)

        def _sage(x, adj, Wr, Wx, b, mf):
            deg = jnp.clip(jnp.sum(adj, axis=-1, keepdims=True), 1.0, None)
            agg = jnp.einsum('bij,bjd->bid', adj, x) / deg
            out = agg @ Wr + x @ Wx + b
            nrm = jnp.maximum(jnp.linalg.norm(out, axis=-1, keepdims=True), NORM_EPS)
            return out / nrm * mf[..., None]

        def _bn(x, g, b):
            m = jnp.mean(x, axis=(0, 1))
            v = jnp.var(x, axis=(0, 1))
            return (x - m) * jax.lax.rsqrt(v + BN_EPS) * g + b

        def _forward(x, adj, mask, Wr1, Wx1, b1, g1, be1, Wr2, Wx2, b2, g2, be2, Wr3, Wx3, b3, g3, be3, Wl, bl):
            mf = mask.astype(x.dtype)
            adj_d = _dilate(adj, mask)
            h1 = _bn(jax.nn.relu(_sage(x, adj_d, Wr1, Wx1, b1, mf)), g1, be1)
            h2 = _bn(jax.nn.relu(_sage(h1, adj_d, Wr2, Wx2, b2, mf)), g2, be2)
            h3 = _bn(jax.nn.relu(_sage(h2, adj_d, Wr3, Wx3, b3, mf)), g3, be3)
            xc = jnp.concatenate([h1, h2, h3], axis=-1) * mf[..., None]
            return (xc @ Wl + bl) * mf[..., None]
        return _forward(x, adj, mask, Wr1, Wx1, b1, g1, be1, Wr2, Wx2, b2, g2, be2, Wr3, Wx3, b3, g3, be3, Wl, bl)

    x = _layernorm(x + _L0_gnn_ref(x, adj, L0_gnn_kernel), axis=-1)
    x = _layernorm(x + _L1_gnn_ref(x, adj, nodemask, L1_gnn_Wr1, L1_gnn_Wx1, L1_gnn_b1, L1_gnn_g1, L1_gnn_be1, L1_gnn_Wr2, L1_gnn_Wx2, L1_gnn_b2, L1_gnn_g2, L1_gnn_be2, L1_gnn_Wr3, L1_gnn_Wx3, L1_gnn_b3, L1_gnn_g3, L1_gnn_be3, L1_gnn_Wl, L1_gnn_bl), axis=-1)
    return x


_drawn_inputs = setup_inputs


def setup_inputs(seed=0):
    import zlib

    import numpy as np

    out = dict(_drawn_inputs(seed))
    spreads = {'L1_gnn_b1': (0.0, 0.1),
     'L1_gnn_g1': (1.0, 0.2),
     'L1_gnn_be1': (0.0, 0.1),
     'L1_gnn_b2': (0.0, 0.1),
     'L1_gnn_g2': (1.0, 0.2),
     'L1_gnn_be2': (0.0, 0.1),
     'L1_gnn_b3': (0.0, 0.1),
     'L1_gnn_g3': (1.0, 0.2),
     'L1_gnn_be3': (0.0, 0.1),
     'L1_gnn_bl': (0.0, 0.1)}
    factors = {}
    for name, (base, spread) in spreads.items():
        noise = np.random.default_rng([zlib.crc32(name.encode()), seed]).standard_normal(out[name].shape)
        drawn = base * np.exp(spread * noise) if base else spread * noise
        out[name] = jnp.asarray(drawn.astype(out[name].dtype))
    for name, factor in factors.items():
        out[name] = (out[name] * factor).astype(out[name].dtype)
    return out
```

```python
import concourse.bass as bass
from concourse import mybir
from contextlib import ExitStack

ALU = mybir.AluOpType
ACT = mybir.ActivationFunctionType
AX = mybir.AxisListType
F32 = mybir.dt.float32
F16 = mybir.dt.float16
U8 = mybir.dt.uint8
I32 = mybir.dt.int32

P = 128
ROUND2 = 1.5 * 2.0 ** 24
CODE = 8192.0


def row(buf, gp, q, lo, hi):
    return buf[:, bass.ds(gp * 2 + q, 1), lo:hi].rearrange("p a c -> p (a c)")


def dilate(nc, adj, mask, keep_rows, keep_cols, adj_sum, maskv):
    G, N, _ = adj.shape
    NB = N // P
    GP = G // 2
    RING = 3
    with ExitStack() as ctx:
        def sb(name, shape, dt):
            return ctx.enter_context(nc.sbuf_tensor(name, shape, dt))

        def ps(name, shape, dt):
            return ctx.enter_context(nc.psum_tensor(name, shape, dt))

        def sem(name):
            return ctx.enter_context(nc.semaphore(name))

        adj_ring = sb("adj_ring", [P, RING, N], F32)
        member = [sb(f"member{i}", [P, G, N], F16) for i in range(2)]
        rank = sb("rank", [P, G, N], F16)
        kept_in = sb("kept_in", [P, G, N - 2 * P], U8)
        kept_out = [sb(f"kept_out{i}", [P, NB, G, P], U8) for i in range(2)]
        away = sb("away", [P, 2, N], F16)
        dist = sb("dist", [P, 2, N], F16)
        kept_row = sb("kept_row", [P, 2, N], U8)
        ones = sb("ones", [P, 1], F16)
        ident = sb("ident", [P, P], F16)
        above = sb("above", [P, P], F16)
        maski = sb("maski", [P, NB, G], I32)
        maskf = sb("maskf", [P, NB, G], F32)
        code = sb("code", [P, G, P], F32)
        pairs = sb("pairs", [P, G, P], F16)
        hit_mid = sb("hit_mid", [P, G, P], F16)
        hit = sb("hit", [P, G, P], F16)
        s = {n: sb("s_" + n, [P, G], F32) for n in
             ("upper", "count0", "dm", "even", "big", "valid", "par", "t_mid", "t_low", "t_low0", "removed", "rold",
              "diff", "count", "odd", "x1", "x2", "x3", "half", "mid", "bias_lo", "bias_up", "goal", "scale")}
        moved = sb("moved", [P, 1], F32)
        onesf = sb("onesf", [P, P], F32)
        flag = sb("flag", [1, 1], I32)

        turned = [ps(f"turned{i}", [P, NB, P], F16) for i in range(2)]
        turned_diag = ps("turned_diag", [P, G, P], F16)
        turned_hit = ps("turned_hit", [P, G, P], F16)
        removed_ps = ps("removed_ps", [P, 512], F32)
        flag_ps = ps("flag_ps", [P, 512], F32)

        consts = sem("consts")
        mask_in = sem("mask_in")
        adj_in = [sem(f"adj_in{i}") for i in range(RING)]
        kept_loaded = sem("kept_loaded")
        kept_stored = sem("kept_stored")
        rows_stored = [sem(f"rows_stored{i}") for i in range(2)]
        signs = sem("signs")
        row_sums = sem("row_sums")
        step = sem("step")
        lower = sem("lower")
        members = sem("members")
        diag_turned = sem("diag_turned")
        hits = sem("hits")
        counted = sem("counted")
        moved_ready = sem("moved_ready")
        flag_counted = sem("flag_counted")
        flag_ready = sem("flag_ready")
        hit_turned = sem("hit_turned")
        ranks = sem("ranks")
        dists = sem("dists")
        aways = sem("aways")
        rows_turned = sem("rows_turned")
        cols_ready = sem("cols_ready")
        rows_ready = sem("rows_ready")

        in_round = sem("in_round")

        def dist_count(t):
            return 2 * min(t, (NB - 1) * G) + max(0, t - (NB - 1) * G)

        block = ctx.enter_context(nc.Block())

        @block.gpsimd
        def _(pool):
            nc.gpsimd.memset(ident[:], 0.0).then_inc(consts, 1)
            nc.gpsimd.memset(above[:], 1.0).then_inc(consts, 1)
            nc.gpsimd.memset(ones[:], 1.0).then_inc(consts, 1)
            nc.gpsimd.memset(onesf[:], 1.0).then_inc(consts, 1)
            pool.wait_ge(consts, 4)
            nc.gpsimd.affine_select(out=ident[:], in_=ident[:], compare_op=ALU.not_equal, fill=1.0, base=0,
                                    pattern=[[-1, P]], channel_multiplier=1).then_inc(consts, 1)
            nc.gpsimd.affine_select(out=above[:], in_=above[:], compare_op=ALU.is_gt, fill=0.0, base=0,
                                    pattern=[[1, P]], channel_multiplier=-1).then_inc(consts, 1)
            for t in range(NB * G):
                pool.wait_ge(aways, t + 1)
                if t >= 2:
                    pool.wait_ge(rows_stored[t % 2], 16 * (t // 2))
                nc.gpsimd.tensor_scalar(kept_row[:, t % 2, :], away[:, t % 2, :], -1.0, 1.0,
                                        ALU.mult, ALU.add).then_inc(rows_ready, 1)

        @block.sync
        def _(sp):
            sp.dma_start(maski[:], mask).then_inc(mask_in, 16)

            def load(b):
                for g in range(G):
                    t = b * G + g
                    if t >= RING:
                        sp.wait_ge(row_sums, t - RING + 1)
                    sp.dma_start(adj_ring[:, t % RING, :], adj[g, b * P:(b + 1) * P, :]).then_inc(adj_in[t % RING], 16)

            load(0)
            for b in range(NB):
                if b + 1 < NB:
                    load(b + 1)
                if 1 <= b < NB - 1:
                    sp.wait_ge(kept_stored, 16 * G * b)
                    if b >= 2:
                        sp.wait_ge(lower, G * (b - 1))
                    sp.dma_start(kept_in[:, :, 0:b * P],
                                 keep_cols[:, (b + 1) * P:(b + 2) * P, 0:b * P].rearrange("g p c -> p g c")
                                 ).then_inc(kept_loaded, 16)
                for g in range(G):
                    t = b * G + g
                    sp.wait_ge(rows_ready, t + 1)
                    sp.dma_start(keep_rows[g, b * P:(b + 1) * P, :], kept_row[:, t % 2, :]).then_inc(rows_stored[t % 2], 16)
                    sp.wait_ge(cols_ready, t + 1)
                    sp.dma_start(keep_cols[g, :, b * P:(b + 1) * P].rearrange("(j p) c -> p j c", p=P),
                                 kept_out[b % 2][:, :, g, :]).then_inc(kept_stored, 16)
            sp.wait_ge(kept_stored, 16 * G * NB)
            for i in range(2):
                sp.wait_ge(rows_stored[i], 16 * G * NB // 2)

        @block.scalar
        def _(act):
            def sign_block(b):
                for g in range(G):
                    t = b * G + g
                    act.wait_ge(adj_in[t % RING], 16 * (t // RING + 1))
                    if b >= 2 and g == 0:
                        act.wait_ge(aways, (b - 1) * G)
                    nc.scalar.activation(member[b % 2][:, g, :], adj_ring[:, t % RING, :], ACT.Sign).then_inc(signs, 1)
                    nc.scalar.activation(adj_ring[:, t % RING, :], adj_ring[:, t % RING, :], ACT.Copy,
                                         accum_out=adj_sum[:, g, b:b + 1]).then_inc(row_sums, 1)

            sign_block(0)
            for b in range(NB):
                if b + 1 < NB:
                    sign_block(b + 1)
                act.wait_ge(ranks, b + 1)
                if b >= 2:
                    act.wait_ge(kept_stored, 16 * G * (b - 1))
                W = (b + 1) * P
                for g in range(G + 1):
                    if g < G:
                        t = b * G + g
                        if t >= 2:
                            act.wait_ge(aways, t - 1)
                        nc.scalar.activation(dist[:, g % 2, 0:W], rank[:, g, 0:W], ACT.Abs,
                                             bias=s["bias_lo"][:, g:g + 1],
                                             scale=s["scale"][:, g:g + 1]).then_inc(dists, 1)
                        if W < N:
                            nc.scalar.activation(dist[:, g % 2, W:N], rank[:, g, W:N], ACT.Abs,
                                                 bias=s["bias_up"][:, g:g + 1],
                                                 scale=s["scale"][:, g:g + 1]).then_inc(dists, 1)
                    if g >= 1:
                        h = g - 1
                        act.wait_ge(rows_turned, b * G + h + 1)
                        nc.scalar.activation(kept_out[b % 2][:, :, h, :], turned[h % 2][:, :, :], ACT.Identity,
                                             scale=-1.0, bias=1.0).then_inc(cols_ready, 1)

        @block.tensor
        def _(pe):
            pe.wait_ge(consts, 6)
            rounds = pe.alloc_register("pe_rounds")
            pe.reg_mov(rounds, 0)
            still = pe.alloc_register("pe_still")
            for b in range(NB):
                pe.wait_ge(members, (b + 1) * G)
                for g in range(G):
                    mm = pe.transpose(turned_diag[:, g, :], member[b % 2][:, g, b * P:(b + 1) * P], ident[:])
                mm.then_inc(diag_turned, 1)
                pe.reg_mov(still, 1)
                with pe.While(lambda: pe.snap(still) != 0):
                    done = pe.snap(rounds)
                    pe.wait_ge(hits, done + 1)
                    for g in range(G):
                        mm = pe.matmul(removed_ps[:, g:g + 1], hit[:, g, :], ones[:], start=True, stop=True)
                    mm.then_inc(counted, 1)
                    pe.wait_ge(moved_ready, done + 1)
                    pe.matmul(flag_ps[0:1, 0:1], moved[:], onesf[:, 0:1], start=True, stop=True).then_inc(flag_counted, 1)
                    pe.wait_ge(flag_ready, done + 1)
                    pe.reg_add(rounds, rounds, 1)
                    pe.reg_load(still, flag[0:1, 0:1])
                for g in range(G):
                    mm = pe.transpose(turned_hit[:, g, :], hit[:, g, :], ident[:])
                mm.then_inc(hit_turned, 1)
                for g in range(G):
                    t = b * G + g
                    pe.wait_ge(aways, t + 1)
                    if t >= 2:
                        pe.wait_ge(cols_ready, t - 1)
                    for j in range(NB):
                        mm = pe.transpose(turned[g % 2][:, j, :], away[:, g % 2, j * P:(j + 1) * P], ident[:])
                    mm.then_inc(rows_turned, 1)

        @block.vector
        def _(dve):
            steps = [0]

            def then(ins):
                steps[0] += 1
                ins.then_inc(step, 1)
                dve.wait_ge(step, steps[0])

            v = nc.vector
            dve.wait_ge(mask_in, 16)
            then(v.tensor_scalar(maskf[:], maski[:], 0.0, None, ALU.not_equal))
            then(v.tensor_copy(maskv[:], maski[:]))
            dve.wait_ge(consts, 6)
            rounds = dve.alloc_register("dve_rounds")
            dve.reg_mov(rounds, 0)
            still = dve.alloc_register("dve_still")

            def bc(t):
                return t[:].rearrange("p (g o) -> p g o", o=1).broadcast_to([P, G, P])

            def static_part(b):
                lo = b * P
                m = member[b % 2]
                for g in range(G):
                    dve.wait_ge(signs, b * G + g + 1)
                    v.tensor_scalar(m[:, g, lo:N], m[:, g, lo:N], 0.0, None, ALU.is_gt).then_inc(members, 1)
                dve.wait_ge(members, (b + 1) * G)
                if b >= 1:
                    dve.wait_ge(dists, dist_count(b * G))
                for g in range(G):
                    v.tensor_tensor_scan(rank[:, g, lo:N], ones[:].broadcast_to([P, N - lo]), m[:, g, lo:N], 0.0, ALU.mult, ALU.add).then_inc(step, 1)
                    steps[0] += 1
                hi = (b - 1) * P
                if b >= 2:
                    dve.wait_ge(kept_loaded, 16 * (b - 1))
                    for g in range(G):
                        v.scalar_tensor_tensor(m[:, g, 0:hi], m[:, g, 0:hi], 0.0, kept_in[:, g, 0:hi], ALU.is_gt, ALU.mult).then_inc(lower, 1)
                    dve.wait_ge(lower, (b - 1) * G)
                    for g in range(G):
                        v.tensor_tensor_scan(rank[:, g, 0:hi], ones[:].broadcast_to([P, hi]), m[:, g, 0:hi], 0.0, ALU.mult, ALU.add).then_inc(step, 1)
                        steps[0] += 1
                dve.wait_ge(step, steps[0])

            static_part(0)
            for b in range(NB):
                lo = b * P
                m = member[b % 2]
                diag = slice(lo, lo + P)
                if b >= 1:
                    last = slice(lo - P, lo)
                    dve.wait_ge(cols_ready, b * G)
                    then(v.scalar_tensor_tensor(m[:, :, last], m[:, :, last], 0.0, kept_out[(b - 1) % 2][:, b, :, :],
                                                ALU.is_gt, ALU.mult))
                    for g in range(G):
                        v.tensor_tensor_scan(rank[:, g, last], ones[:].broadcast_to([P, P]), m[:, g, last],
                                             rank[:, g, lo - P - 1:lo - P] if b >= 2 else 0.0, ALU.mult, ALU.add).then_inc(step, 1)
                        steps[0] += 1
                    dve.wait_ge(step, steps[0])
                v.tensor_copy(s["upper"][:], rank[:, :, N - 1:N].rearrange("p g o -> p (g o)")).then_inc(step, 1)
                steps[0] += 1
                dve.wait_ge(step, steps[0])
                if b >= 1:
                    then(v.tensor_tensor(s["count0"][:], s["upper"][:], rank[:, :, lo - 1:lo].rearrange("p g o -> p (g o)"), ALU.add))
                else:
                    then(v.tensor_copy(s["count0"][:], s["upper"][:]))
                then(v.scalar_tensor_tensor(code[:], rank[:, :, diag], 1.0, bc(s["upper"]), ALU.mult, ALU.subtract))
                then(v.tensor_scalar(code[:], code[:], 2.0, CODE + 1.0, ALU.mult, ALU.add))
                dve.wait_ge(diag_turned, b + 1)
                then(v.tensor_tensor(pairs[:], m[:, :, diag], above[:].rearrange("p (o c) -> p o c", o=1).broadcast_to([P, G, P]), ALU.mult))
                then(v.tensor_tensor(pairs[:], pairs[:], turned_diag[:], ALU.mult))
                then(v.tensor_tensor(code[:], code[:], pairs[:], ALU.mult))
                then(v.tensor_scalar(code[:], code[:], -1.0, None, ALU.add))
                then(v.memset(s["removed"][:], 0.0))
                dve.reg_mov(still, 1)
                with dve.While(lambda: dve.snap(still) != 0):
                    inner = in_round
                    done = dve.snap(rounds)
                    k = [0]
                    K = 13

                    def link(ins):
                        k[0] += 1
                        ins.then_inc(inner, 1)
                        dve.wait_ge(inner, done * K + k[0])

                    link(v.scalar_tensor_tensor(s["dm"][:], s["count0"][:], -0.5, s["removed"][:], ALU.add, ALU.subtract))
                    link(v.tensor_scalar(s["even"][:], s["dm"][:], ROUND2, -ROUND2, ALU.add, ALU.add))
                    link(v.tensor_scalar(s["big"][:], s["dm"][:], 10.0, None, ALU.is_ge))
                    link(v.scalar_tensor_tensor(s["valid"][:], s["dm"][:], 1.0, maskf[:, b, :], ALU.is_ge, ALU.mult))
                    link(v.tensor_tensor(s["big"][:], s["big"][:], maskf[:, b, :], ALU.mult))
                    link(v.scalar_tensor_tensor(s["par"][:], s["dm"][:], 9500.0, s["even"][:], ALU.add, ALU.subtract))
                    link(v.scalar_tensor_tensor(s["t_mid"][:], s["big"][:], CODE, s["even"][:], ALU.mult, ALU.subtract))
                    link(v.scalar_tensor_tensor(s["t_low0"][:], s["valid"][:], -9498.0, s["par"][:], ALU.mult, ALU.add))
                    link(v.scalar_tensor_tensor(s["t_low"][:], s["big"][:], 8190.5, s["t_low0"][:], ALU.mult, ALU.add))
                    link(v.tensor_tensor(hit_mid[:], code[:], bc(s["t_mid"]), ALU.is_equal))
                    link(v.tensor_tensor(hit[:], code[:], bc(s["t_low"]), ALU.is_ge))
                    v.tensor_tensor(hit[:], hit[:], hit_mid[:], ALU.add).then_inc(hits, 1)
                    dve.wait_ge(counted, done + 1)
                    link(v.tensor_tensor(s["diff"][:], removed_ps[:, 0:G], s["removed"][:], ALU.not_equal))
                    v.tensor_reduce(moved[:], s["diff"][:], AX.X, ALU.add).then_inc(moved_ready, 1)
                    link(v.tensor_copy(s["removed"][:], removed_ps[:, 0:G]))
                    assert k[0] == K
                    dve.wait_ge(flag_counted, done + 1)
                    v.tensor_copy(flag[:], flag_ps[0:1, 0:1]).then_inc(flag_ready, 1)
                    dve.wait_ge(flag_ready, done + 1)
                    dve.reg_add(rounds, rounds, 1)
                    dve.reg_load(still, flag[0:1, 0:1])
                dve.wait_ge(hit_turned, b + 1)
                then(v.scalar_tensor_tensor(m[:, :, diag], turned_hit[:], 0.0, m[:, :, diag], ALU.is_equal, ALU.mult))
                for g in range(G):
                    v.tensor_tensor_scan(rank[:, g, diag], ones[:].broadcast_to([P, P]), m[:, g, diag],
                                         rank[:, g, lo - 1:lo] if b >= 1 else 0.0, ALU.mult, ALU.add).then_inc(step, 1)
                    steps[0] += 1
                then(v.tensor_scalar(s["count"][:], s["dm"][:], 0.5, None, ALU.add))
                then(v.tensor_tensor(s["odd"][:], s["count"][:], s["even"][:], ALU.subtract))
                then(v.scalar_tensor_tensor(s["x1"][:], s["odd"][:], 0.0, s["count"][:], ALU.is_equal, ALU.mult))
                then(v.tensor_tensor(s["x1"][:], s["x1"][:], s["odd"][:], ALU.add))
                then(v.tensor_scalar(s["half"][:], s["x1"][:], 0.25, None, ALU.mult))
                then(v.tensor_tensor(s["x2"][:], s["count"][:], s["odd"][:], ALU.add))
                then(v.scalar_tensor_tensor(s["mid"][:], s["x2"][:], 0.5, s["half"][:], ALU.mult, ALU.add))
                then(v.scalar_tensor_tensor(s["x3"][:], s["mid"][:], 1.0, s["big"][:], ALU.add, ALU.mult))
                then(v.tensor_scalar(s["bias_lo"][:], s["x3"][:], -1.0, 1.0, ALU.mult, ALU.add))
                then(v.tensor_tensor(s["x1"][:], s["count"][:], s["upper"][:], ALU.subtract))
                then(v.tensor_tensor(s["x1"][:], s["x1"][:], s["big"][:], ALU.mult))
                then(v.tensor_tensor(s["bias_up"][:], s["bias_lo"][:], s["x1"][:], ALU.add))
                then(v.scalar_tensor_tensor(s["x2"][:], s["half"][:], 1.0, s["big"][:], ALU.subtract, ALU.mult))
                then(v.tensor_scalar(s["x3"][:], s["valid"][:], 2.0, -1.0, ALU.mult, ALU.add))
                then(v.tensor_tensor(s["goal"][:], s["x2"][:], s["x3"][:], ALU.add))
                v.tensor_copy(s["scale"][:], s["big"][:]).then_inc(ranks, 1)
                for g in range(G):
                    t = b * G + g
                    dve.wait_ge(dists, dist_count(t + 1))
                    if t >= 2:
                        dve.wait_ge(rows_turned, t - 1)
                        dve.wait_ge(rows_ready, t - 1)
                    v.scalar_tensor_tensor(away[:, g % 2, :], dist[:, g % 2, :], s["goal"][:, g:g + 1], m[:, g, :],
                                           ALU.is_equal, ALU.mult).then_inc(aways, 1)
                if b + 1 < NB:
                    static_part(b + 1)



def rows4(t):
    return t[:].rearrange("p (a c) -> p a c", a=4)


def first_layers(nc, adj_t, x, x_diag, params, keep_rows, keep_cols, adj_sum, maskf, sums, adj_kept, x1_dram, r_dram, deg_keep):
    G, N, _ = adj_t.shape
    NB = N // P
    NQ = N // 512
    with ExitStack() as ctx:
        def sb(name, shape, dt):
            return ctx.enter_context(nc.sbuf_tensor(name, shape, dt))

        def sem(name):
            return ctx.enter_context(nc.semaphore(name))

        adjt = sb("adjt", [P, NB, N], F32)
        kr = sb("kr", [P, 2, N], U8)
        kc = sb("kc", [P, 2, N], U8)
        xin = sb("xin", [P, NB, P], F32)
        ybuf = sb("ybuf", [P, NB, P], F32)
        zbuf = sb("zbuf", [P, NB, P], F32)
        obuf = sb("obuf", [P, NB, P], F32)
        agg_t = sb("agg_t", [P, N], F32)
        deg_acc = sb("deg_acc", [P, N], F32)
        w = sb("w", [P, 4, P], F32)
        ident = sb("identf", [P, P], F32)
        ones = sb("ones_f", [P, P], F32)
        sq_row = sb("sq_row", [P, 512], F32)
        diag = sb("diag", [P, G, NB], F32)
        dinv = sb("dinv", [P, G, NB], F32)
        rest = sb("rest", [P, G, NB], F32)
        t_a = sb("t_a", [P, NB], F32)
        t_b = sb("t_b", [P, NB], F32)
        t_c = sb("t_c", [P, NB], F32)
        acc = [ctx.enter_context(nc.psum_tensor(f"acc{i}", [P, 512], F32)) for i in range(NQ)]
        pe_a = [ctx.enter_context(nc.psum_tensor(f"pe_a{i}", [P, 512], F32)) for i in range(2)]
        pe_x = [ctx.enter_context(nc.psum_tensor(f"pe_x{i}", [P, 512], F32)) for i in range(2)]

        consts = sem("b_consts")
        params_in = sem("b_params_in")
        x_in = sem("x_in")
        adjt_in = [sem(f"adjt_in{j}") for j in range(NB)]
        keep_in = [sem(f"keep_in{i}") for i in range(2)]
        step = sem("b_step")
        scaled = sem("scaled")
        raw_used = sem("raw_used")
        acc0_done = sem("acc0_done")
        agg0_ready = sem("agg0_ready")
        w0_done = sem("w0_done")
        w0_read = sem("w0_read")
        masked = sem("masked")
        deg_added = sem("deg_added")
        sqrt_in = sem("sqrt_in")
        sqrt_out = sem("sqrt_out")
        x1_ready = sem("x1_ready")
        x1_turned = sem("x1_turned")
        x1t_ready = sem("x1t_ready")
        main_used = sem("main_used")
        agg1_ready = sem("agg1_ready")
        deg_done = sem("deg_done")
        deg_read = sem("deg_read")
        out_done = sem("out_done")
        out_read = sem("out_read")
        r_ready = sem("r_ready")
        r_summed = sem("r_summed")
        kept_stored = [sem(f"b_kept_stored{j}") for j in range(NB)]
        x1_stored = sem("x1_stored")
        r_stored = sem("r_stored")
        pool_step = sem("pool_step")

        block = ctx.enter_context(nc.Block())

        def wait(eng, s, value):
            if value > 0:
                eng.wait_ge(s, value)

        @block.sync
        def _(sp):
            sp.dma_start(w[:], params[:, 0:4, :]).then_inc(params_in, 16)
            sp.dma_start(diag[:], x_diag).then_inc(params_in, 16)

            def load_x(g):
                wait(sp, x1_ready, g)
                sp.dma_start(xin[:], x[g]).then_inc(x_in, 16)

            def load_adj(g, j):
                wait(sp, kept_stored[j], 16 * g)
                wait(sp, main_used, (g - 1) * NB + j + 1)
                wait(sp, deg_added, (g - 1) * NB + j + 1)
                sp.dma_start(adjt[:, j, :], adj_t[g, j * P:(j + 1) * P, :]).then_inc(adjt_in[j], 16)

            load_x(0)
            for j in range(NB):
                load_adj(0, j)
            for g in range(G):
                for j in range(NB):
                    wait(sp, masked, g * NB + j - 1)
                    sp.dma_start(kr[:, j % 2, :], keep_rows[g, j * P:(j + 1) * P, :]).then_inc(keep_in[j % 2], 16)
                    sp.dma_start(kc[:, j % 2, :], keep_cols[g, j * P:(j + 1) * P, :]).then_inc(keep_in[j % 2], 16)
                if g + 1 < G:
                    load_x(g + 1)
                    for j in range(NB):
                        load_adj(g + 1, j)

        @block.gpsimd
        def _(pool):
            nc.gpsimd.memset(ident[:], 0.0).then_inc(consts, 1)
            nc.gpsimd.memset(ones[:], 1.0).then_inc(consts, 1)
            nc.gpsimd.memset(sums[:], 0.0).then_inc(consts, 1)
            pool.wait_ge(consts, 3)
            nc.gpsimd.affine_select(out=ident[:], in_=ident[:], compare_op=ALU.not_equal, fill=1.0, base=0,
                                    pattern=[[-1, P]], channel_multiplier=1).then_inc(consts, 1)
            steps = [0]

            def then(ins):
                steps[0] += 1
                ins.then_inc(pool_step, 1)
                pool.wait_ge(pool_step, steps[0])

            for g in range(G):
                for j in range(NB):
                    pool.wait_ge(masked, g * NB + j + 1)
                    if j == 0:
                        wait(pool, deg_done, g)
                        nc.gpsimd.tensor_copy(deg_acc[:], adjt[:, j, :]).then_inc(deg_added, 1)
                    else:
                        pool.wait_ge(deg_added, g * NB + j)
                        nc.gpsimd.tensor_tensor(deg_acc[:], deg_acc[:], adjt[:, j, :], ALU.add).then_inc(deg_added, 1)
                pool.wait_ge(r_ready, g + 1)
                for q in range(NQ):
                    r = obuf[:, 4 * q:4 * q + 4, :].rearrange("p a c -> p (a c)")
                    then(nc.gpsimd.tensor_tensor(sums[:, 0, :], sums[:, 0, :], r, ALU.add))
                    then(nc.gpsimd.tensor_tensor(sq_row[:], r, r, ALU.mult))
                    then(nc.gpsimd.tensor_tensor(sums[:, 1, :], sums[:, 1, :], sq_row[:], ALU.add))
                nc.gpsimd.tensor_copy(sq_row[:, 0:1], sq_row[:, 0:1]).then_inc(r_summed, 1)

        @block.scalar
        def _(act):
            act.wait_ge(sqrt_in, 1)
            nc.scalar.activation(dinv[:], dinv[:], ACT.Sqrt).then_inc(sqrt_out, 1)
            for g in range(G):
                act.wait_ge(acc0_done, g + 1)
                wait(act, r_ready, g)
                for q in range(NQ):
                    nc.scalar.activation(agg_t[:, 512 * q:512 * q + 512], acc[q][:], ACT.Copy).then_inc(agg0_ready, 1)
                act.wait_ge(sqrt_in, 2 * g + 2)
                nc.scalar.activation(t_a[:], t_b[:], ACT.Sqrt).then_inc(sqrt_out, 1)
                act.wait_ge(x1_ready, g + 1)
                act.dma_start(x1_dram[g], ybuf[:]).then_inc(x1_stored, 16)
                for q in range(NQ):
                    act.wait_ge(x1_turned, g * NQ + q + 1)
                    nc.scalar.activation(zbuf[:, 4 * q:4 * q + 4, :], rows4(pe_a[q % 2]), ACT.Copy).then_inc(x1t_ready, 1)
                for j in range(NB):
                    act.wait_ge(masked, g * NB + j + 1)
                    act.dma_start(adj_kept[g, j * P:(j + 1) * P, :], adjt[:, j, :]).then_inc(kept_stored[j], 16)
                act.wait_ge(main_used, (g + 1) * NB)
                act.wait_ge(w0_done, (g + 1) * NQ)
                for q in range(NQ):
                    nc.scalar.activation(agg_t[:, 512 * q:512 * q + 512], acc[q][:], ACT.Copy).then_inc(agg1_ready, 1)
                act.wait_ge(sqrt_in, 2 * g + 3)
                nc.scalar.activation(t_a[:], t_b[:], ACT.Sqrt).then_inc(sqrt_out, 1)
                act.wait_ge(r_ready, g + 1)
                act.dma_start(r_dram[g], obuf[:]).then_inc(r_stored, 16)
            for j in range(NB):
                act.wait_ge(kept_stored[j], 16 * G)
            act.wait_ge(x1_stored, 16 * G)
            act.wait_ge(r_stored, 16 * G)

        @block.tensor
        def _(pe):
            pe.wait_ge(consts, 4)
            pe.wait_ge(params_in, 32)
            w0, wr, wx, bias = (w[:, i, :] for i in range(4))
            for g in range(G):
                pe.wait_ge(scaled, g + 1)
                wait(pe, agg1_ready, g * NQ)
                for j in range(NB):
                    pe.wait_ge(adjt_in[j], 16 * (g + 1))
                    for q in range(NQ):
                        mm = pe.matmul(acc[q][:], ybuf[:, j, :], adjt[:, j, 512 * q:512 * q + 512], start=(j == 0), stop=False)
                    mm.then_inc(raw_used, 1)
                for j in range(NB):
                    mm = pe.matmul(acc[j // 4][:, (j % 4) * P:(j % 4 + 1) * P], zbuf[:, j, :], ident[:], start=False,
                                   stop=(j % 4 == 3))
                mm.then_inc(acc0_done, 1)
                for q in range(NQ):
                    pe.wait_ge(agg0_ready, g * NQ + q + 1)
                    wait(pe, w0_read, g * NQ + q - 1)
                    if q < 2:
                        wait(pe, out_read, g * NQ)
                    for a in range(4):
                        i = 4 * q + a
                        mm = pe.matmul(pe_x[q % 2][:, a * P:(a + 1) * P], agg_t[:, i * P:(i + 1) * P], w0, start=True, stop=True)
                    mm.then_inc(w0_done, 1)
                pe.wait_ge(x1_ready, g + 1)
                for q in range(NQ):
                    wait(pe, x1t_ready, g * NQ + q - 1)
                    for a in range(4):
                        mm = pe.transpose(pe_a[q % 2][:, a * P:(a + 1) * P], ybuf[:, 4 * q + a, :], ident[:])
                    mm.then_inc(x1_turned, 1)
                for j in range(NB):
                    pe.wait_ge(masked, g * NB + j + 1)
                    if j == 0:
                        pe.wait_ge(agg0_ready, (g + 1) * NQ)
                    for q in range(NQ):
                        mm = pe.matmul(acc[q][:], ybuf[:, j, :], adjt[:, j, 512 * q:512 * q + 512], start=(j == 0), stop=(j == NB - 1))
                    mm.then_inc(main_used, 1)
                pe.wait_ge(deg_added, (g + 1) * NB)
                pe.wait_ge(w0_read, (g + 1) * NQ)
                for i in range(NB):
                    mm = pe.matmul(pe_x[0][:, i:i + 1], deg_acc[:, i * P:(i + 1) * P], ones[:, 0:1], start=True, stop=True)
                mm.then_inc(deg_done, 1)
                pe.wait_ge(deg_read, g + 1)
                pe.wait_ge(x1t_ready, (g + 1) * NQ)
                for q in range(NQ):
                    pe.wait_ge(agg1_ready, g * NQ + q + 1)
                    wait(pe, out_read, g * NQ + q - 1)
                    for a in range(4):
                        i = 4 * q + a
                        cols = slice(a * P, (a + 1) * P)
                        pe.matmul(pe_a[q % 2][:, cols], agg_t[:, i * P:(i + 1) * P], wr, start=True, stop=True)
                        pe.matmul(pe_x[q % 2][:, cols], zbuf[:, i, :], wx, start=True, stop=False)
                        mm = pe.matmul(pe_x[q % 2][:, cols], ones[0:1, :], bias[0:1, :], start=False, stop=True)
                    mm.then_inc(out_done, 1)

        @block.vector
        def _(dve):
            v = nc.vector
            steps = [0]

            def then(ins):
                steps[0] += 1
                ins.then_inc(step, 1)
                dve.wait_ge(step, steps[0])

            def bc(t, n=NB):
                return t.rearrange("p (g o) -> p g o", o=1).broadcast_to([P, n, P])

            dve.wait_ge(params_in, 32)
            then(v.tensor_scalar(rest[:], diag[:], -1.0, 1.0, ALU.mult, ALU.add))
            v.tensor_tensor(dinv[:], adj_sum[:], rest[:], ALU.add).then_inc(sqrt_in, 1)
            dve.wait_ge(sqrt_out, 1)
            then(v.tensor_scalar(dinv[:], dinv[:], 1e-6, None, ALU.add))
            then(v.reciprocal(dinv[:], dinv[:]))
            for g in range(G):
                dg = dinv[:, g, :]
                dve.wait_ge(x_in, 16 * (g + 1))
                wait(dve, main_used, g * NB)
                wait(dve, x1_stored, 16 * g)
                wait(dve, out_done, g * NQ)
                then(v.tensor_tensor(ybuf[:], xin[:], bc(dg), ALU.mult))
                v.tensor_tensor(zbuf[:], ybuf[:], bc(rest[:, g, :]), ALU.mult).then_inc(scaled, 1)
                for j in range(NB):
                    dve.wait_ge(keep_in[j % 2], 32 * (g * (NB // 2) + j // 2 + 1))
                    dve.wait_ge(raw_used, g * NB + j + 1)
                    k32 = kr[:, j % 2, :].bitcast(I32)
                    then(v.tensor_tensor(k32, k32, kc[:, j % 2, :].bitcast(I32), ALU.bitwise_and))
                    v.scalar_tensor_tensor(adjt[:, j, :], adjt[:, j, :], 0.0, kr[:, j % 2, :], ALU.max, ALU.mult).then_inc(masked, 1)
                wait(dve, r_stored, 16 * g)
                wait(dve, r_summed, g)
                for q in range(NQ):
                    dve.wait_ge(w0_done, g * NQ + q + 1)
                    o = obuf[:, 4 * q:4 * q + 4, :]
                    v.scalar_tensor_tensor(o, rows4(pe_x[q % 2]), 0.0, bc(dg[:, 4 * q:4 * q + 4], 4), ALU.max, ALU.mult).then_inc(w0_read, 1)
                dve.wait_ge(w0_read, (g + 1) * NQ)
                then(v.tensor_tensor(obuf[:], obuf[:], xin[:], ALU.add))
                then(v.tensor_reduce(t_c[:], obuf[:], AX.X, ALU.add))
                then(v.tensor_scalar(t_c[:], t_c[:], -1.0 / P, None, ALU.mult))
                then(v.tensor_tensor(obuf[:], obuf[:], bc(t_c[:]), ALU.add))
                dve.wait_ge(acc0_done, g + 1)
                then(v.tensor_tensor(zbuf[:], obuf[:], obuf[:], ALU.mult))
                then(v.tensor_reduce(t_b[:], zbuf[:], AX.X, ALU.add))
                v.tensor_scalar(t_b[:], t_b[:], 1.0 / P, 1e-5, ALU.mult, ALU.add).then_inc(sqrt_in, 1)
                dve.wait_ge(sqrt_out, 2 * g + 2)
                then(v.reciprocal(t_a[:], t_a[:]))
                v.tensor_tensor(ybuf[:], obuf[:], bc(t_a[:]), ALU.mult).then_inc(x1_ready, 1)
                dve.wait_ge(deg_done, g + 1)
                v.tensor_scalar(t_c[:], pe_x[0][:, 0:NB], 1.0, None, ALU.max).then_inc(deg_read, 1)
                dve.wait_ge(deg_read, g + 1)
                v.reciprocal(deg_keep[:, g, :], t_c[:]).then_inc(step, 1)
                steps[0] += 1
                dve.wait_ge(step, steps[0])
                norm_rows(nc, dve, then, bc, g, NQ, out_done, out_read, pe_a, pe_x, obuf, agg_t, deg_keep, maskf,
                          t_a, t_b, sqrt_in, 2 * g + 3, sqrt_out, r_ready)


def norm_rows(nc, dve, then, bc, g, NQ, out_done, out_read, pe_a, pe_x, obuf, scratch, deg_keep, maskf, t_a, t_b,
              sqrt_in, sqrt_n, sqrt_out, r_ready, out_n=None):
    v = nc.vector
    out_n = g * NQ if out_n is None else out_n
    for q in range(NQ):
        dve.wait_ge(out_done, out_n + q + 1)
        o = obuf[:, 4 * q:4 * q + 4, :]
        then(v.tensor_tensor(o, rows4(pe_a[q % 2]), bc(deg_keep[:, g, 4 * q:4 * q + 4], 4), ALU.mult))
        v.tensor_tensor(o, o, rows4(pe_x[q % 2]), ALU.add).then_inc(out_read, 1)
    dve.wait_ge(out_read, out_n + NQ)
    sq = scratch[:].rearrange("p (a c) -> p a c", c=P)
    then(v.tensor_tensor(sq, obuf[:], obuf[:], ALU.mult))
    v.tensor_reduce(t_b[:], sq, AX.X, ALU.add).then_inc(sqrt_in, 1)
    dve.wait_ge(sqrt_out, sqrt_n)
    then(v.tensor_scalar(t_a[:], t_a[:], 1e-12, None, ALU.max))
    then(v.reciprocal(t_a[:], t_a[:]))
    then(v.tensor_tensor(t_a[:], t_a[:], maskf[:, :, g], ALU.mult))
    then(v.tensor_tensor(obuf[:], obuf[:], bc(t_a[:]), ALU.mult))
    v.tensor_scalar(obuf[:], obuf[:], 0.0, None, ALU.max).then_inc(r_ready, 1)


def last_layers(nc, params, maskf, sums, adj_kept, x1_dram, r_dram, deg_keep, out):
    G, N, _ = adj_kept.shape
    NB = N // P
    NQ = N // 512
    RING = 8
    with ExitStack() as ctx:
        def sb(name, shape, dt):
            return ctx.enter_context(nc.sbuf_tensor(name, shape, dt))

        def sem(name):
            return ctx.enter_context(nc.semaphore(name))

        ring = sb("ring", [P, RING, N], F32)
        y = sb("y", [P, G, NB, P], F32)
        hbuf = [sb(f"hbuf{i}", [P, NB, P], F32) for i in range(2)]
        h_t = [sb(f"h_t{i}", [P, NB, P], F32) for i in range(2)]
        agg_t = sb("agg_t2", [P, N], F32)
        obuf = sb("obuf2", [P, NB, P], F32)
        w = sb("w2", [P, 16, P], F32)
        ident = sb("ident2", [P, P], F32)
        ones = sb("ones2", [P, P], F32)
        sq_row = sb("sq_row2", [P, 512], F32)
        gain = sb("gain", [P, P], F32)
        shift = sb("shift", [P, P], F32)
        mean = sb("mean", [P, P], F32)
        var = sb("var", [P, P], F32)
        t_a = sb("t_a2", [P, NB], F32)
        t_b = sb("t_b2", [P, NB], F32)
        t_c = sb("t_c2", [P, NB], F32)
        acc = [ctx.enter_context(nc.psum_tensor(f"acc2{i}", [P, 512], F32)) for i in range(NQ)]
        pe_a = [ctx.enter_context(nc.psum_tensor(f"pe_a2{i}", [P, 512], F32)) for i in range(2)]
        pe_x = [ctx.enter_context(nc.psum_tensor(f"pe_x2{i}", [P, 512], F32)) for i in range(2)]

        consts = sem("c_consts")
        params_in = sem("c_params_in")
        r_in = [sem(f"r_in{i}") for i in range(2)]
        tile_in = [sem(f"tile_in{i}") for i in range(RING)]
        step = sem("c_step")
        pool_step = sem("c_pool_step")
        summed = sem("summed")
        sqrt_in = sem("c_sqrt_in")
        sqrt_out = sem("c_sqrt_out")
        h_ready = sem("h_ready")
        h_turned = sem("h_turned")
        h_t_ready = sem("h_t_ready")
        y_done = sem("y_done")
        y_read = sem("y_read")
        tile_used = sem("tile_used")
        agg_ready = sem("agg_ready")
        out_done = sem("c_out_done")
        out_read = sem("c_out_read")
        r_ready = sem("c_r_ready")
        r_summed = sem("c_r_summed")
        r_stored = sem("c_r_stored")
        x1_in = sem("x1_in")
        fin_ready = sem("fin_ready")
        out_stored = sem("out_stored")
        block = ctx.enter_context(nc.Block())

        def wait(eng, s, value):
            if value > 0:
                eng.wait_ge(s, value)

        @block.sync
        def _(sp):
            sp.dma_start(w[:], params[:, 4:20, :]).then_inc(params_in, 16)

            def load_r(n):
                layer, g = divmod(n, G)
                wait(sp, tile_used, (n - 1) * NB if layer < 2 else min(n - 1, 2 * G) * NB)
                wait(sp, h_turned, (n - 1) * NQ)
                if layer >= 1:
                    sp.wait_ge(r_stored, 16 * (n - G + 1))
                sp.dma_start(hbuf[n % 2][:], r_dram[g]).then_inc(r_in[n % 2], 16)

            load_r(0)
            for layer in range(2):
                for g in range(G):
                    n = layer * G + g
                    for j in range(NB):
                        t = n * NB + j
                        wait(sp, tile_used, t - RING + 1)
                        sp.dma_start(ring[:, t % RING, :], adj_kept[g, j * P:(j + 1) * P, :]).then_inc(tile_in[t % RING], 16)
                        if j == 1 and g + 1 < G:
                            load_r(n + 1)
                load_r((layer + 1) * G)
            for g in range(G):
                n = 2 * G + g
                wait(sp, fin_ready, g)
                if g > 0:
                    sp.wait_ge(out_stored, 16 * g)
                if g == 0:
                    sp.wait_ge(r_stored, 16 * 2 * G)
                    sp.wait_ge(r_summed, 2 * G)
                sp.dma_start(obuf[:], x1_dram[g]).then_inc(x1_in, 16)
                if g + 1 < G:
                    load_r(n + 1)
                sp.wait_ge(fin_ready, g + 1)
                sp.dma_start(out[g], obuf[:]).then_inc(out_stored, 16)
            sp.wait_ge(out_stored, 16 * G)

        @block.gpsimd
        def _(pool):
            nc.gpsimd.memset(ident[:], 0.0).then_inc(consts, 1)
            nc.gpsimd.memset(ones[:], 1.0).then_inc(consts, 1)
            pool.wait_ge(consts, 2)
            nc.gpsimd.affine_select(out=ident[:], in_=ident[:], compare_op=ALU.not_equal, fill=1.0, base=0,
                                    pattern=[[-1, P]], channel_multiplier=1).then_inc(consts, 1)
            steps = [0]

            def then(ins):
                steps[0] += 1
                ins.then_inc(pool_step, 1)
                pool.wait_ge(pool_step, steps[0])

            for layer in range(2):
                pool.wait_ge(summed, layer + 1)
                then(nc.gpsimd.memset(sums[:], 0.0))
                for g in range(G):
                    n = layer * G + g
                    pool.wait_ge(r_ready, n + 1)
                    for q in range(NQ):
                        r = obuf[:, 4 * q:4 * q + 4, :].rearrange("p a c -> p (a c)")
                        then(nc.gpsimd.tensor_tensor(sums[:, 0, :], sums[:, 0, :], r, ALU.add))
                        then(nc.gpsimd.tensor_tensor(sq_row[:], r, r, ALU.mult))
                        then(nc.gpsimd.tensor_tensor(sums[:, 1, :], sums[:, 1, :], sq_row[:], ALU.add))
                    nc.gpsimd.tensor_copy(sq_row[:, 0:1], sq_row[:, 0:1]).then_inc(r_summed, 1)

        @block.scalar
        def _(act):
            sqrts = [0]

            def root(dst, src):
                sqrts[0] += 1
                act.wait_ge(sqrt_in, sqrts[0])
                nc.scalar.activation(dst, src, ACT.Sqrt).then_inc(sqrt_out, 1)

            def turn(n):
                for q in range(NQ):
                    act.wait_ge(h_turned, n * NQ + q + 1)
                    if q == 0 and n >= 2:
                        act.wait_ge(out_done, min(n - 1, 2 * G) * NQ)
                        act.wait_ge(y_done, (n - 1) * NQ)
                    nc.scalar.activation(h_t[n % 2][:, 4 * q:4 * q + 4, :], rows4(pe_a[q % 2]), ACT.Copy).then_inc(h_t_ready, 1)

            for layer in range(2):
                root(var[:], var[:])
                turn(layer * G)
                for g in range(G):
                    n = layer * G + g
                    act.wait_ge(tile_used, (n + 1) * NB)
                    wait(act, r_ready, n)
                    for q in range(NQ):
                        nc.scalar.activation(agg_t[:, 512 * q:512 * q + 512], acc[q][:], ACT.Copy).then_inc(agg_ready, 1)
                    if g + 1 < G:
                        turn(n + 1)
                    root(t_a[:], t_b[:])
                    act.wait_ge(r_ready, n + 1)
                    act.dma_start(r_dram[g], obuf[:]).then_inc(r_stored, 16)
            root(var[:], var[:])
            for g in range(G):
                turn(2 * G + g)
                root(t_a[:], t_b[:])
            act.wait_ge(r_stored, 16 * 2 * G)

        @block.tensor
        def _(pe):
            pe.wait_ge(consts, 3)
            pe.wait_ge(params_in, 16)

            def batch_sums(layer):
                if layer == 0:
                    pass
                else:
                    pe.wait_ge(r_summed, layer * G)
                    pe.wait_ge(out_read, layer * G * NQ)
                for i in range(2):
                    for a in range(4):
                        mm = pe.matmul(pe_x[0][:, i * P:(i + 1) * P], ones[:], sums[:, i, a * P:(a + 1) * P],
                                       start=(a == 0), stop=(a == 3))
                mm.then_inc(summed, 1)

            def prep(n):
                layer, g = divmod(n, G)
                wl = w[:, 9 + layer, :]
                pe.wait_ge(h_ready, n + 1)
                for q in range(NQ):
                    wait(pe, h_t_ready, n * NQ + q - 1)
                    wait(pe, out_read, min(max(n - 1, 0), 2 * G) * NQ if g > 0 else min(n, 2 * G) * NQ)
                    for a in range(4):
                        mm = pe.transpose(pe_a[q % 2][:, a * P:(a + 1) * P], hbuf[n % 2][:, 4 * q + a, :], ident[:])
                    mm.then_inc(h_turned, 1)
                for q in range(NQ):
                    pe.wait_ge(h_t_ready, n * NQ + q + 1)
                    wait(pe, y_read, n * NQ + q - 1)
                    for a in range(4):
                        mm = pe.matmul(pe_x[q % 2][:, a * P:(a + 1) * P], h_t[n % 2][:, 4 * q + a, :], wl, start=True, stop=True)
                    mm.then_inc(y_done, 1)

            for layer in range(2):
                wr, wx, bias = (w[:, 3 * layer + i, :] for i in range(3))
                batch_sums(layer)
                prep(layer * G)
                for g in range(G):
                    n = layer * G + g
                    wait(pe, agg_ready, n * NQ)
                    for j in range(NB):
                        t = n * NB + j
                        pe.wait_ge(tile_in[t % RING], 16 * (t // RING + 1))
                        for q in range(NQ):
                            mm = pe.matmul(acc[q][:], hbuf[n % 2][:, j, :], ring[:, t % RING, 512 * q:512 * q + 512],
                                           start=(j == 0), stop=(j == NB - 1))
                        mm.then_inc(tile_used, 1)
                    if g + 1 < G:
                        prep(n + 1)
                        pe.wait_ge(h_t_ready, (n + 2) * NQ)
                        pe.wait_ge(y_read, (n + 2) * NQ)
                    else:
                        pe.wait_ge(h_t_ready, (n + 1) * NQ)
                        pe.wait_ge(y_read, (n + 1) * NQ)
                    for q in range(NQ):
                        pe.wait_ge(agg_ready, n * NQ + q + 1)
                        wait(pe, out_read, n * NQ + q - 1)
                        for a in range(4):
                            i = 4 * q + a
                            cols = slice(a * P, (a + 1) * P)
                            pe.matmul(pe_a[q % 2][:, cols], agg_t[:, i * P:(i + 1) * P], wr, start=True, stop=True)
                            pe.matmul(pe_x[q % 2][:, cols], h_t[n % 2][:, i, :], wx, start=True, stop=False)
                            mm = pe.matmul(pe_x[q % 2][:, cols], ones[0:1, :], bias[0:1, :], start=False, stop=True)
                        mm.then_inc(out_done, 1)
            batch_sums(2)
            for g in range(G):
                prep(2 * G + g)

        @block.vector
        def _(dve):
            v = nc.vector
            steps = [0]
            sqrts = [0]

            def then(ins):
                steps[0] += 1
                ins.then_inc(step, 1)
                dve.wait_ge(step, steps[0])

            def bc(t, n=NB):
                return t.rearrange("p (g o) -> p g o", o=1).broadcast_to([P, n, P])

            def bcm(t, n=NB):
                return t.rearrange("p (o c) -> p o c", o=1).broadcast_to([P, n, P])

            def batch_norm(layer):
                M = 1.0 / (G * N)
                dve.wait_ge(summed, layer + 1)
                then(v.tensor_scalar(mean[:], pe_x[0][:, 0:P], M, None, ALU.mult))
                then(v.tensor_tensor(gain[:], mean[:], mean[:], ALU.mult))
                then(v.scalar_tensor_tensor(var[:], pe_x[0][:, P:2 * P], M, gain[:], ALU.mult, ALU.subtract))
                then(v.tensor_scalar(var[:], var[:], 0.0, None, ALU.max))
                sqrts[0] += 1
                v.tensor_scalar(var[:], var[:], 1e-5, None, ALU.add).then_inc(sqrt_in, 1)
                dve.wait_ge(sqrt_out, sqrts[0])
                then(v.reciprocal(gain[:], var[:]))
                then(v.tensor_tensor(gain[:], gain[:], gains[layer], ALU.mult))
                then(v.tensor_tensor(shift[:], mean[:], gain[:], ALU.mult))
                then(v.tensor_tensor(shift[:], shifts[layer], shift[:], ALU.subtract))

            gains = [w[:, i, :] for i in (6, 12, 14)]
            shifts = [w[:, i, :] for i in (7, 13, 15)]

            def normalize(n):
                dve.wait_ge(r_in[n % 2], 16 * (n // 2 + 1))
                h = hbuf[n % 2]
                then(v.tensor_tensor(h[:], h[:], bcm(gain[:]), ALU.mult))
                v.tensor_tensor(h[:], h[:], bcm(shift[:]), ALU.add).then_inc(h_ready, 1)

            def add_y(n):
                layer, g = divmod(n, G)
                for q in range(NQ):
                    dve.wait_ge(y_done, n * NQ + q + 1)
                    yq = y[:, g, 4 * q:4 * q + 4, :]
                    if layer == 0:
                        v.tensor_copy(yq, rows4(pe_x[q % 2])).then_inc(y_read, 1)
                    else:
                        v.tensor_tensor(yq, yq, rows4(pe_x[q % 2]), ALU.add).then_inc(y_read, 1)

            dve.wait_ge(params_in, 16)
            for layer in range(2):
                batch_norm(layer)
                normalize(layer * G)
                add_y(layer * G)
                for g in range(G):
                    n = layer * G + g
                    if g + 1 < G:
                        normalize(n + 1)
                        add_y(n + 1)
                    wait(dve, r_stored, 16 * n)
                    wait(dve, r_summed, n)
                    sqrts[0] += 1
                    norm_rows(nc, dve, then, bc, g, NQ, out_done, out_read, pe_a, pe_x, obuf, agg_t, deg_keep, maskf,
                              t_a, t_b, sqrt_in, sqrts[0], sqrt_out, r_ready, out_n=n * NQ)
            batch_norm(2)
            for g in range(G):
                n = 2 * G + g
                normalize(n)
                add_y(n)
                dve.wait_ge(y_read, (n + 1) * NQ)
                yg = y[:, g]
                mg = maskf[:, :, g]
                dve.wait_ge(x1_in, 16 * (g + 1))
                then(v.tensor_tensor(yg, yg, bc(mg), ALU.mult))
                then(v.tensor_tensor(yg, yg, bcm(w[:, 8, :]), ALU.add))
                then(v.tensor_tensor(yg, yg, bc(mg), ALU.mult))
                then(v.tensor_tensor(yg, yg, obuf[:], ALU.add))
                then(v.tensor_reduce(t_c[:], yg, AX.X, ALU.add))
                then(v.tensor_scalar(t_c[:], t_c[:], -1.0 / P, None, ALU.mult))
                then(v.tensor_tensor(yg, yg, bc(t_c[:]), ALU.add))
                sq = agg_t[:].rearrange("p (a c) -> p a c", c=P)
                then(v.tensor_tensor(sq, yg, yg, ALU.mult))
                then(v.tensor_reduce(t_b[:], sq, AX.X, ALU.add))
                sqrts[0] += 1
                v.tensor_scalar(t_b[:], t_b[:], 1.0 / P, 1e-5, ALU.mult, ALU.add).then_inc(sqrt_in, 1)
                dve.wait_ge(sqrt_out, sqrts[0])
                then(v.reciprocal(t_a[:], t_a[:]))
                v.tensor_tensor(obuf[:], yg, bc(t_a[:]), ALU.mult).then_inc(fin_ready, 1)


def program(nc, adj, adj_t, mask, x, x_diag, params, out):
    G, N, _ = adj.shape
    NB = N // P

    def scratch(name, shape, dt):
        return nc.dram_tensor(name, shape, dt).ap()

    keep_rows = scratch("keep_rows", (G, N, N), U8)
    keep_cols = scratch("keep_cols", (G, N, N), U8)
    adj_kept = scratch("adj_kept", (G, N, N), F32)
    x1_dram = scratch("x1_dram", (G, P, NB, P), F32)
    r_dram = scratch("r_dram", (G, P, NB, P), F32)
    with ExitStack() as ctx:
        adj_sum = ctx.enter_context(nc.sbuf_tensor("adj_sum", [P, G, NB], F32))
        maskv = ctx.enter_context(nc.sbuf_tensor("maskv", [P, NB, G], F32))
        deg_keep = ctx.enter_context(nc.sbuf_tensor("deg_keep", [P, G, NB], F32))
        sums = ctx.enter_context(nc.sbuf_tensor("sums", [P, 2, 512], F32))
        dilate(nc, adj, mask, keep_rows, keep_cols, adj_sum, maskv)
        first_layers(nc, adj_t, x, x_diag, params, keep_rows, keep_cols, adj_sum, maskv, sums, adj_kept, x1_dram,
                     r_dram, deg_keep)
        last_layers(nc, params, maskv, sums, adj_kept, x1_dram, r_dram, deg_keep, out)


def kernel(**inputs):
    import numpy as _np
    import concourse.bacc as _bacc
    from concourse import mybir as _mybir
    from concourse.bass_utils import run_bass_kernel_spmd as _run

    adj, x, mask = (_np.asarray(inputs[n]) for n in ("adj", "x", "nodemask"))
    G, N, D = x.shape
    NB = N // P

    def weight(name):
        return _np.asarray(inputs[name]).reshape(-1, P, D)

    def spread(name):
        return _np.broadcast_to(_np.asarray(inputs["L1_gnn_" + name]), (1, P, D))

    params = _np.concatenate(
        [weight("L0_gnn_kernel"), weight("L1_gnn_Wr1"), weight("L1_gnn_Wx1"), spread("b1"),
         weight("L1_gnn_Wr2"), weight("L1_gnn_Wx2"), spread("b2"), weight("L1_gnn_Wr3"), weight("L1_gnn_Wx3"),
         spread("b3"), spread("g1"), spread("be1"), spread("bl"), weight("L1_gnn_Wl"),
         spread("g2"), spread("be2"), spread("g3"), spread("be3")]).transpose(1, 0, 2)
    laid_out = {
        "adj": adj,
        "adj_t": adj.transpose(0, 2, 1),
        "mask": mask.reshape(G, NB, P).transpose(2, 1, 0),
        "x": x.reshape(G, NB, P, D).transpose(0, 2, 1, 3),
        "x_diag": _np.diagonal(adj, axis1=1, axis2=2).reshape(G, NB, P).transpose(2, 0, 1),
        "params": params,
    }
    nc = _bacc.Bacc("TRN2", target_bir_lowering=False, num_devices=1)
    arrays, args = {}, []
    for name, a in laid_out.items():
        a = _np.ascontiguousarray(a)
        arrays[f"in_{name}_dram"] = a
        args.append(nc.dram_tensor(f"in_{name}_dram", a.shape, _mybir.dt.from_np(a.dtype), kind="ExternalInput").ap())
    args.append(nc.dram_tensor("out_dram", (G, P, NB, D), F32, kind="ExternalOutput").ap())
    program(nc, *args)
    r = _run(nc, [arrays], core_ids=[0])
    return r.results[0]["out_dram"].transpose(0, 2, 1, 3).reshape(G, N, D)
```

```python
import concourse.bass as bass
from concourse import mybir
from contextlib import ExitStack

ALU = mybir.AluOpType
ACT = mybir.ActivationFunctionType
AX = mybir.AxisListType
F32 = mybir.dt.float32
F16 = mybir.dt.float16
U8 = mybir.dt.uint8
I8 = mybir.dt.int8
I32 = mybir.dt.int32

P = 128
ROUND2 = 1.5 * 2.0 ** 24
CODE = 8192.0


def row(buf, gp, q, lo, hi):
    return buf[:, bass.ds(gp * 2 + q, 1), lo:hi].rearrange("p a c -> p (a c)")


def rows4(t):
    return t[:].rearrange("p (a c) -> p a c", a=4)


def over_columns(t, n, width=P):
    return t.rearrange("p (g o) -> p g o", o=1).broadcast_to([P, n, width])


def over_blocks(t, n):
    return t.rearrange("p (o c) -> p o c", o=1).broadcast_to([P, n, t.shape[1]])


def dilate(nc, adj, adj_t, mask, x, x_diag, params, keep, removed_cols, u_dram, maskv):
    G, N, _ = adj.shape
    NB = N // P
    NQ = N // 512
    HB = NB // 2
    RING = 3
    TRING = 3
    AWAY = 3
    LAG = 3
    with ExitStack() as ctx:
        def sb(name, shape, dt):
            return ctx.enter_context(nc.sbuf_tensor(name, shape, dt))

        def ps(name, shape, dt):
            return ctx.enter_context(nc.psum_tensor(name, shape, dt))

        def sem(name):
            return ctx.enter_context(nc.semaphore(name))

        adj_ring = sb("adj_ring", [P, RING, N], F32)
        member = [sb(f"member{i}", [P, G, N], I8) for i in range(2)]
        own = [sb(f"own{i}", [P, G, P], F16) for i in range(2)]
        rank = sb("rank", [P, G, N], F16)
        removed_in = [sb(f"removed_in{i}", [P, G, N - (3 - i) * P], U8) for i in range(2)]
        cols_out = sb("cols_out", [P, NB, G, P], U8)
        keep_own = sb("keep_own", [P, G, P], U8)
        away = sb("away", [P, AWAY, N], F16)
        keep_row = sb("keep_row", [P, 2, N - P], U8)
        ones = sb("ones", [P, 1], F16)
        ident = sb("ident", [P, P], F16)
        above = sb("above", [P, P], F16)
        maski = sb("maski", [P, NB, G], I32)
        maskf = sb("maskf", [P, NB, G], F32)
        code = sb("code", [P, G, P], F32)
        pairs = sb("pairs", [P, G, P], F16)
        hit_mid = sb("hit_mid", [P, G, P], F16)
        hit = sb("hit", [P, G, P], F16)
        own_gone = hit_mid
        s = {n: sb("s_" + n, [P, G], F32) for n in
             ("upper", "count0", "dm", "even", "big", "valid", "par", "t_mid", "t_low", "t_low0", "removed",
              "diff", "count", "odd", "x1", "x2", "x3", "half", "mid", "bias_lo", "bias_up", "goal", "scale")}
        moved = sb("moved", [P, 1], F32)
        onesf = sb("onesf", [P, 1], F32)
        flag = sb("flag", [1, 1], I32)
        tile_ring = sb("tile_ring", [P, TRING, N], F32)
        xin = sb("xin", [P, NB, P], F32)
        ybuf = sb("ybuf", [P, NB, P], F32)
        w0 = sb("w0", [P, P], F32)
        diag = sb("diag", [P, G, NB], F32)
        adj_sum = sb("adj_sum", [P, G, NB], F32)
        dinv = sb("dinv", [P, G, NB], F32)

        turned = [ps(f"turned{i}", [P, HB, P], F16) for i in range(2)]
        turned_own = ps("turned_own", [P, G, P], F16)
        count_ps = ps("count_ps", [P, 512], F32)
        acc = [ps(f"acc{i}", [P, 512], F32) for i in range(NQ)]
        removed_ps = count_ps[:, 0:G]
        flag_ps = count_ps[0:1, 2 * G:2 * G + 1]

        consts = sem("consts")
        mask_in = sem("mask_in")
        params_in = sem("params_in")
        adj_in = [sem(f"adj_in{i}") for i in range(RING)]
        adj_read = sem("adj_read")
        own_ready = sem("own_ready")
        members = sem("members")
        removed_loaded = sem("removed_loaded")
        cols_stored = sem("cols_stored")
        joined = sem("joined")
        own_saved = sem("own_saved")
        own_kept = sem("own_kept")
        own_stored = sem("own_stored")
        rows_stored = [sem(f"rows_stored{i}") for i in range(2)]
        step = sem("step")
        pool_step = sem("pool_step")
        lower = sem("lower")
        own_turned = sem("own_turned")
        pairs_ready = sem("pairs_ready")
        in_round = sem("in_round")
        hits = sem("hits")
        counted = sem("counted")
        moved_ready = sem("moved_ready")
        flag_counted = sem("flag_counted")
        flag_ready = sem("flag_ready")
        hit_turned = sem("hit_turned")
        ranks = sem("ranks")
        dists = sem("dists")
        aways = sem("aways")
        rows_turned = sem("rows_turned")
        cols_ready = sem("cols_ready")
        rows_ready = sem("rows_ready")
        degrees = sem("degrees")
        roots = sem("roots")
        dinv_ready = sem("dinv_ready")
        x_in = sem("x_in")
        y_ready = sem("y_ready")
        tile_in = [sem(f"tile_in{i}") for i in range(TRING)]
        tile_ready = sem("tile_ready")
        tile_used = sem("tile_used")
        agg_ready = sem("agg_ready")
        w0_done = sem("w0_done")
        relu_ready = sem("relu_ready")
        u_ready = sem("u_ready")
        u_stored = sem("u_stored")

        def dist_count(t):
            return 2 * min(t, (NB - 1) * G) + max(0, t - (NB - 1) * G)

        def half_sums(u):
            return [("sum", u // 2, (u % 2) * HB + j) for j in range(HB)]

        reads = {(-1, 0): [("sign", 0, g) for g in range(G)]}
        for b in range(NB):
            reads[b, 0] = [("sign", b + 1, g) for g in range(G)] if b + 1 < NB else []
            if b == 0:
                reads[b, 0] += half_sums(0) + half_sums(1)
            reads[b, 1] = half_sums(b + 2) if b + 2 < NB else []
        first_read, n_read = {}, 0
        for key, tiles in reads.items():
            first_read[key] = n_read
            n_read += len(tiles)

        def sign_count(b, g):
            return first_read[b - 1, 0] + g + 1

        def agg_t(h):
            return tile_ring[:, (h + 1) * NB % TRING, :]

        def copies(b):
            cut = b + 1
            return [(i, lo, hi, kept) for i in range(2)
                    for lo, hi, kept in ((i * HB, min(cut, (i + 1) * HB), True), (max(cut, i * HB), (i + 1) * HB, False))
                    if lo < hi]

        def copied(t, half=0):
            b, g = divmod(t, G)
            return (G * sum(len(copies(i)) for i in range(b)) + (g * len(copies(b)) if g else 0)
                    + (sum(c[0] < half for c in copies(b)) if half else 0))

        def join_count(t):
            return max(0, min(t, 2 * G) - G) + 2 * max(0, t - 2 * G)

        def stores(b):
            return sum((i >= 1) + (i + 2 < NB) for i in range(b)) * G

        block = ctx.enter_context(nc.Block())

        def wait(eng, s, value):
            if value > 0:
                eng.wait_ge(s, value)

        @block.sync
        def _(sp):
            sp.dma_start(maski[:], mask).then_inc(mask_in, 16)

            def load_reads(key, some=slice(None)):
                for i, (kind, m, n) in list(enumerate(reads[key]))[some]:
                    t = first_read[key] + i
                    rows, g = (m, n) if kind == "sign" else (n, m)
                    wait(sp, adj_read, t - RING + 1)
                    sp.dma_start(adj_ring[:, t % RING, :], adj[g, rows * P:(rows + 1) * P, :]).then_inc(adj_in[t % RING], 16)

            load_reads((-1, 0))
            sp.dma_start(w0[:], params[:, 0, :]).then_inc(params_in, 16)
            sp.dma_start(diag[:], x_diag).then_inc(params_in, 16)
            for b in range(NB):
                if 1 <= b < NB - 1:
                    sp.wait_ge(cols_stored, 16 * stores(b))
                    wait(sp, joined, join_count(b * G))
                    sp.dma_start(removed_in[(b + 1) % 2][:, :, 0:b * P],
                                 removed_cols[:, (b + 1) * P:(b + 2) * P, 0:b * P].rearrange("g p c -> p g c")
                                 ).then_inc(removed_loaded, 16)
                load_reads((b, 0))
                if b % 2 == 0:
                    wait(sp, u_ready, b // 2)
                    sp.dma_start(xin[:], x[b // 2]).then_inc(x_in, 16)
                for j in range(HB):
                    t = b * HB + j
                    rows = (b % 2) * HB + j
                    wait(sp, tile_used, t - TRING + 1)
                    if rows == 0:
                        wait(sp, w0_done, b // 2 * NQ)
                    sp.dma_start(tile_ring[:, t % TRING, :], adj_t[b // 2, rows * P:(rows + 1) * P, :]).then_inc(tile_in[t % TRING], 16)
                    load_reads((b, 1), slice(j, j + 1))

        @block.gpsimd
        def _(pool):
            nc.gpsimd.memset(ident[:], 0.0).then_inc(consts, 1)
            nc.gpsimd.memset(above[:], 1.0).then_inc(consts, 1)
            nc.gpsimd.memset(ones[:], 1.0).then_inc(consts, 1)
            nc.gpsimd.memset(onesf[:], 1.0).then_inc(consts, 1)
            pool.wait_ge(consts, 4)
            nc.gpsimd.affine_select(out=ident[:], in_=ident[:], compare_op=ALU.not_equal, fill=1.0, base=0,
                                    pattern=[[-1, P]], channel_multiplier=1).then_inc(consts, 1)
            nc.gpsimd.affine_select(out=above[:], in_=above[:], compare_op=ALU.is_gt, fill=0.0, base=0,
                                    pattern=[[1, P]], channel_multiplier=-1).then_inc(consts, 1)

            def store_own(b):
                lo = b * P
                pool.wait_ge(own_kept, b + 1)
                pool.dma_start(keep[:, lo:lo + P, lo:lo + P].rearrange("g p c -> p g c"), keep_own[:]).then_inc(own_stored, 16)

            for b in range(NB):
                lo = b * P
                if b >= 1:
                    store_own(b - 1)
                for g in range(G):
                    t = b * G + g
                    pool.wait_ge(aways, t + 1)
                    nc.gpsimd.tensor_copy(own_gone[:, g, :], away[:, t % AWAY, lo:lo + P]).then_inc(own_saved, 1)
                    if b >= 1:
                        r = t - G
                        pool.wait_ge(joined, join_count(t + 1))
                        wait(pool, rows_stored[r % 2], 16 * (r // 2))
                        nc.gpsimd.tensor_scalar(keep_row[:, r % 2, 0:lo], away[:, t % AWAY, 0:lo], -1.0, 1.0,
                                                ALU.mult, ALU.add).then_inc(rows_ready, 1)
                        pool.wait_ge(rows_ready, r + 1)
                        pool.dma_start(keep[g, lo:lo + P, 0:lo], keep_row[:, r % 2, 0:lo]).then_inc(rows_stored[r % 2], 16)
                h = b // 2
                if b % 2 == 0:
                    pool.wait_ge(dinv_ready, h + 1)
                    pool.wait_ge(x_in, 16 * (h + 1))
                    wait(pool, u_stored, 16 * h)
                    nc.gpsimd.tensor_tensor(ybuf[:], xin[:], over_columns(dinv[:, h, :], NB), ALU.mult).then_inc(y_ready, 1)
                for j in range(HB):
                    t = b * HB + j
                    rows = (b % 2) * HB + j
                    pool.wait_ge(tile_in[t % TRING], 16 * (t // TRING + 1))
                    own_cols = tile_ring[:, t % TRING, rows * P:(rows + 1) * P]
                    nc.gpsimd.affine_select(out=own_cols, in_=own_cols, compare_op=ALU.not_equal, fill=1.0, base=0,
                                            pattern=[[-1, P]], channel_multiplier=1).then_inc(tile_ready, 1)
                if b % 2 == 1:
                    pool.wait_ge(relu_ready, (h + 1) * NB)
                    nc.gpsimd.tensor_tensor(ybuf[:], ybuf[:], xin[:], ALU.add).then_inc(u_ready, 1)
                    pool.wait_ge(u_ready, h + 1)
                    pool.dma_start(u_dram[h], ybuf[:]).then_inc(u_stored, 16)
            pool.wait_ge(u_stored, 16 * G)
            store_own(NB - 1)
            pool.wait_ge(own_stored, 16 * NB)
            for i in range(2):
                pool.wait_ge(rows_stored[i], 16 * G * (NB - 1) // 2)

        @block.scalar
        def _(act):
            def read(key):
                for i, (kind, m, n) in enumerate(reads[key]):
                    t = first_read[key] + i
                    tile = adj_ring[:, t % RING, :]
                    act.wait_ge(adj_in[t % RING], 16 * (t // RING + 1))
                    if kind == "sign":
                        if n == 0:
                            wait(act, aways, (m - 1) * G)
                        nc.scalar.activation(member[m % 2][:, n, :], tile, ACT.Sign).then_inc(adj_read, 1)
                    else:
                        nc.scalar.activation(tile, tile, ACT.Copy, accum_out=adj_sum[:, m, n:n + 1]).then_inc(adj_read, 1)

            read((-1, 0))
            for b in range(NB):
                read((b, 0))
                h = b // 2
                if b % 2 == 0:
                    act.wait_ge(degrees, h + 1)
                    nc.scalar.activation(dinv[:, h, :], dinv[:, h, :], ACT.Sqrt).then_inc(roots, 1)
                act.wait_ge(ranks, b + 1)
                W = (b + 1) * P
                for g in range(G + LAG):
                    if g < G:
                        nc.scalar.activation(rank[:, g, 0:W], rank[:, g, 0:W], ACT.Abs, bias=s["bias_lo"][:, g:g + 1],
                                             scale=s["scale"][:, g:g + 1]).then_inc(dists, 1)
                        if W < N:
                            nc.scalar.activation(rank[:, g, W:N], rank[:, g, W:N], ACT.Abs, bias=s["bias_up"][:, g:g + 1],
                                                 scale=s["scale"][:, g:g + 1]).then_inc(dists, 1)
                    if g >= LAG:
                        d = g - LAG
                        t = b * G + d
                        if d == 0 and b >= 1:
                            act.wait_ge(cols_stored, 16 * stores(b))
                            act.wait_ge(own_kept, b)
                        wait(act, joined, join_count(t + 1))
                        for i, first, end, kept in copies(b):
                            act.wait_ge(rows_turned, 2 * t + i + 1)
                            nc.scalar.activation(cols_out[:, first:end, d, :], turned[i][:, first - i * HB:end - i * HB, :],
                                                 ACT.Identity, scale=-1.0 if kept else 1.0,
                                                 bias=1.0 if kept else 0.0).then_inc(cols_ready, 1)
                        act.wait_ge(cols_ready, copied(t + 1))
                        if b >= 1:
                            act.dma_start(keep[d, 0:b * P, b * P:(b + 1) * P].rearrange("(j p) c -> p j c", p=P),
                                          cols_out[:, 0:b, d, :]).then_inc(cols_stored, 16)
                        if b + 2 < NB:
                            act.dma_start(removed_cols[d, (b + 2) * P:, b * P:(b + 1) * P].rearrange("(j p) c -> p j c", p=P),
                                          cols_out[:, b + 2:, d, :]).then_inc(cols_stored, 16)
                read((b, 1))
                if b % 2 == 1:
                    act.wait_ge(tile_used, (b + 1) * HB)
                    for q in range(NQ):
                        nc.scalar.activation(agg_t(h)[:, 512 * q:512 * q + 512], acc[q][:], ACT.Copy).then_inc(agg_ready, 1)
                    for i in range(NB):
                        if i % 4 == 0:
                            act.wait_ge(w0_done, h * NQ + i // 4 + 1)
                        nc.scalar.activation(ybuf[:, i, :], acc[i // 4][:, (i % 4) * P:(i % 4 + 1) * P], ACT.Relu,
                                             scale=dinv[:, h, i:i + 1]).then_inc(relu_ready, 1)
            act.wait_ge(cols_stored, 16 * stores(NB))

        @block.tensor
        def _(pe):
            pe.wait_ge(consts, 6)
            pe.wait_ge(params_in, 32)
            rounds = pe.alloc_register("pe_rounds")
            pe.reg_mov(rounds, 0)
            still = pe.alloc_register("pe_still")
            for b in range(NB):
                pe.wait_ge(own_ready, b + 1)
                for g in range(G):
                    mm = pe.transpose(turned_own[:, g, :], own[b % 2][:, g, :], ident[:])
                mm.then_inc(own_turned, 1)
                pe.reg_mov(still, 1)
                with pe.While(lambda: pe.snap(still) != 0):
                    done = pe.snap(rounds)
                    pe.wait_ge(hits, done + 1)
                    for g in range(G):
                        mm = pe.matmul(removed_ps[:, g:g + 1], hit[:, g, :], ones[:], start=True, stop=True)
                    mm.then_inc(counted, 1)
                    pe.wait_ge(moved_ready, done + 1)
                    pe.matmul(flag_ps, moved[:], onesf[:], start=True, stop=True).then_inc(flag_counted, 1)
                    pe.wait_ge(flag_ready, done + 1)
                    pe.reg_add(rounds, rounds, 1)
                    pe.reg_load(still, flag[0:1, 0:1])
                for g in range(G):
                    mm = pe.transpose(turned_own[:, g, :], hit[:, g, :], ident[:])
                mm.then_inc(hit_turned, 1)
                for g in range(G):
                    t = b * G + g
                    pe.wait_ge(aways, t + 1)
                    for i in range(2):
                        if t > 0:
                            pe.wait_ge(cols_ready, copied(t - 1, i + 1) if i == 0 else copied(t))
                        if b > i * HB:
                            pe.wait_ge(joined, join_count(t + 1))
                        for j in range(HB):
                            c = i * HB + j
                            mm = pe.transpose(turned[i][:, j, :], away[:, t % AWAY, c * P:(c + 1) * P], ident[:])
                        mm.then_inc(rows_turned, 1)
                h = b // 2
                pe.wait_ge(y_ready, h + 1)
                for j in range(HB):
                    t = b * HB + j
                    rows = (b % 2) * HB + j
                    pe.wait_ge(tile_ready, t + 1)
                    if rows == 0:
                        wait(pe, relu_ready, h * NB)
                    for q in range(NQ):
                        mm = pe.matmul(acc[q][:], ybuf[:, rows, :], tile_ring[:, t % TRING, 512 * q:512 * q + 512],
                                       start=(rows == 0), stop=(rows == NB - 1))
                    mm.then_inc(tile_used, 1)
                if b % 2 == 1:
                    for q in range(NQ):
                        pe.wait_ge(agg_ready, h * NQ + q + 1)
                        for a in range(4):
                            i = 4 * q + a
                            mm = pe.matmul(acc[q][:, a * P:(a + 1) * P], agg_t(h)[:, i * P:(i + 1) * P], w0[:], start=True, stop=True)
                        mm.then_inc(w0_done, 1)

        @block.vector
        def _(dve):
            steps = [0]

            def then(ins):
                steps[0] += 1
                ins.then_inc(step, 1)
                dve.wait_ge(step, steps[0])

            v = nc.vector
            dve.wait_ge(mask_in, 16)
            then(v.tensor_scalar(maskf[:], maski[:], 0.0, None, ALU.not_equal))
            then(v.tensor_copy(maskv[:], maski[:]))
            dve.wait_ge(params_in, 32)
            then(v.tensor_scalar(diag[:], diag[:], -1.0, 1.0, ALU.mult, ALU.add))
            dve.wait_ge(consts, 6)
            rounds = dve.alloc_register("dve_rounds")
            dve.reg_mov(rounds, 0)
            still = dve.alloc_register("dve_still")

            def bc(t):
                return over_columns(t[:], G)

            def scan(g, cols, m, start):
                width = cols.stop - cols.start
                v.tensor_tensor_scan(rank[:, g, cols], ones[:].broadcast_to([P, width]), m[:, g, cols], start,
                                     ALU.mult, ALU.add).then_inc(step, 1)
                steps[0] += 1

            def static_part(b):
                m = member[b % 2]
                for g in range(G):
                    dve.wait_ge(adj_read, sign_count(b, g))
                    v.tensor_scalar(m[:, g, b * P:N], m[:, g, b * P:N], 0.0, None, ALU.max).then_inc(members, 1)
                dve.wait_ge(members, (b + 1) * G)
                v.tensor_copy(own[b % 2][:], m[:, :, b * P:(b + 1) * P]).then_inc(own_ready, 1)
                for g in range(G):
                    wait(dve, aways, (b - 1) * G + g + 1)
                    scan(g, slice(b * P, N), m, 0.0)
                if b >= 2:
                    dve.wait_ge(removed_loaded, 16 * (b - 1))
                    before = slice(0, (b - 1) * P)
                    for g in range(G):
                        v.tensor_tensor(m[:, g, before], m[:, g, before], removed_in[b % 2][:, g, before],
                                        ALU.is_gt).then_inc(lower, 1)
                    dve.wait_ge(lower, (b - 1) * G)
                    for g in range(G):
                        scan(g, before, m, 0.0)
                dve.wait_ge(step, steps[0])

            def keep_own_cols(b):
                dve.wait_ge(cols_ready, copied((b + 1) * G))
                dve.wait_ge(own_saved, (b + 1) * G)
                wait(dve, own_stored, 16 * b)
                v.scalar_tensor_tensor(keep_own[:], own_gone[:], 0.0, cols_out[:, b, :, :], ALU.is_equal,
                                       ALU.mult).then_inc(own_kept, 1)

            static_part(0)
            for b in range(NB):
                lo = b * P
                m = member[b % 2]
                diag_cols = slice(lo, lo + P)
                if b >= 1:
                    last = slice(lo - P, lo)
                    dve.wait_ge(cols_ready, copied(b * G))
                    then(v.tensor_tensor(m[:, :, last], m[:, :, last], cols_out[:, b, :, :], ALU.is_gt))
                    for g in range(G):
                        scan(g, last, m, rank[:, g, lo - P - 1:lo - P] if b >= 2 else 0.0)
                    dve.wait_ge(step, steps[0])
                if b >= 1:
                    keep_own_cols(b - 1)
                then(v.tensor_copy(s["upper"][:], rank[:, :, N - 1:N].rearrange("p g o -> p (g o)")))
                if b >= 1:
                    then(v.tensor_tensor(s["count0"][:], s["upper"][:], rank[:, :, lo - 1:lo].rearrange("p g o -> p (g o)"), ALU.add))
                else:
                    then(v.tensor_copy(s["count0"][:], s["upper"][:]))
                then(v.tensor_tensor(code[:], rank[:, :, diag_cols], bc(s["upper"]), ALU.subtract))
                then(v.tensor_scalar(code[:], code[:], 2.0, CODE + 1.0, ALU.mult, ALU.add))
                dve.wait_ge(own_ready, b + 1)
                then(v.tensor_tensor(pairs[:], own[b % 2][:], over_blocks(above[:], G), ALU.mult))
                dve.wait_ge(own_turned, b + 1)
                then(v.tensor_tensor(pairs[:], pairs[:], turned_own[:], ALU.mult))
                then(v.tensor_tensor(code[:], code[:], pairs[:], ALU.mult))
                then(v.tensor_scalar(code[:], code[:], -1.0, None, ALU.add))
                then(v.memset(s["removed"][:], 0.0))
                dve.reg_mov(still, 1)
                with dve.While(lambda: dve.snap(still) != 0):
                    done = dve.snap(rounds)
                    K = 13
                    k = [0]

                    def link(ins):
                        k[0] += 1
                        ins.then_inc(in_round, 1)
                        dve.wait_ge(in_round, done * K + k[0])

                    link(v.scalar_tensor_tensor(s["dm"][:], s["count0"][:], -0.5, s["removed"][:], ALU.add, ALU.subtract))
                    link(v.tensor_scalar(s["even"][:], s["dm"][:], ROUND2, -ROUND2, ALU.add, ALU.add))
                    link(v.tensor_scalar(s["big"][:], s["dm"][:], 10.0, None, ALU.is_ge))
                    link(v.scalar_tensor_tensor(s["valid"][:], s["dm"][:], 1.0, maskf[:, b, :], ALU.is_ge, ALU.mult))
                    link(v.tensor_tensor(s["big"][:], s["big"][:], maskf[:, b, :], ALU.mult))
                    link(v.scalar_tensor_tensor(s["par"][:], s["dm"][:], 9500.0, s["even"][:], ALU.add, ALU.subtract))
                    link(v.scalar_tensor_tensor(s["t_mid"][:], s["big"][:], CODE, s["even"][:], ALU.mult, ALU.subtract))
                    link(v.scalar_tensor_tensor(s["t_low0"][:], s["valid"][:], -9498.0, s["par"][:], ALU.mult, ALU.add))
                    link(v.scalar_tensor_tensor(s["t_low"][:], s["big"][:], 8190.5, s["t_low0"][:], ALU.mult, ALU.add))
                    link(v.tensor_tensor(hit_mid[:], code[:], bc(s["t_mid"]), ALU.is_equal))
                    link(v.tensor_tensor(hit[:], code[:], bc(s["t_low"]), ALU.is_ge))
                    v.tensor_tensor(hit[:], hit[:], hit_mid[:], ALU.add).then_inc(hits, 1)
                    dve.wait_ge(counted, done + 1)
                    link(v.tensor_tensor(s["diff"][:], removed_ps, s["removed"][:], ALU.not_equal))
                    link(v.tensor_copy(s["removed"][:], removed_ps))
                    v.tensor_reduce(moved[:], s["diff"][:], AX.X, ALU.add).then_inc(moved_ready, 1)
                    assert k[0] == K
                    dve.wait_ge(flag_counted, done + 1)
                    v.tensor_copy(flag[:], flag_ps).then_inc(flag_ready, 1)
                    dve.wait_ge(flag_ready, done + 1)
                    dve.reg_add(rounds, rounds, 1)
                    dve.reg_load(still, flag[0:1, 0:1])
                dve.wait_ge(hit_turned, b + 1)
                then(v.scalar_tensor_tensor(m[:, :, diag_cols], turned_own[:], 0.0, m[:, :, diag_cols], ALU.is_equal, ALU.mult))
                for g in range(G):
                    scan(g, diag_cols, m, rank[:, g, lo - 1:lo] if b >= 1 else 0.0)
                then(v.tensor_scalar(s["count"][:], s["dm"][:], 0.5, None, ALU.add))
                then(v.tensor_tensor(s["odd"][:], s["count"][:], s["even"][:], ALU.subtract))
                then(v.scalar_tensor_tensor(s["x1"][:], s["odd"][:], 0.0, s["count"][:], ALU.is_equal, ALU.mult))
                then(v.tensor_tensor(s["x1"][:], s["x1"][:], s["odd"][:], ALU.add))
                then(v.tensor_scalar(s["half"][:], s["x1"][:], 0.25, None, ALU.mult))
                then(v.tensor_tensor(s["x2"][:], s["count"][:], s["odd"][:], ALU.add))
                then(v.scalar_tensor_tensor(s["mid"][:], s["x2"][:], 0.5, s["half"][:], ALU.mult, ALU.add))
                then(v.scalar_tensor_tensor(s["x3"][:], s["mid"][:], 1.0, s["big"][:], ALU.add, ALU.mult))
                then(v.tensor_scalar(s["bias_lo"][:], s["x3"][:], -1.0, 1.0, ALU.mult, ALU.add))
                then(v.tensor_tensor(s["x1"][:], s["count"][:], s["upper"][:], ALU.subtract))
                then(v.tensor_tensor(s["x1"][:], s["x1"][:], s["big"][:], ALU.mult))
                then(v.tensor_tensor(s["bias_up"][:], s["bias_lo"][:], s["x1"][:], ALU.add))
                then(v.scalar_tensor_tensor(s["x2"][:], s["half"][:], 1.0, s["big"][:], ALU.subtract, ALU.mult))
                then(v.tensor_scalar(s["x3"][:], s["valid"][:], 2.0, -1.0, ALU.mult, ALU.add))
                then(v.tensor_tensor(s["goal"][:], s["x2"][:], s["x3"][:], ALU.add))
                v.tensor_copy(s["scale"][:], s["big"][:]).then_inc(ranks, 1)
                h = b // 2
                if b % 2 == 0:
                    dve.wait_ge(adj_read, first_read[max(b - 1, 0), int(b > 0)] + len(reads[max(b - 1, 0), int(b > 0)]))
                    v.tensor_tensor(dinv[:, h, :], adj_sum[:, h, :], diag[:, h, :], ALU.add).then_inc(degrees, 1)
                for g in range(G + 1):
                    t = b * G + g
                    if g < G:
                        dve.wait_ge(dists, dist_count(t + 1))
                        wait(dve, rows_turned, 2 * (t - AWAY + 1))
                        wait(dve, own_saved, t - AWAY + 1)
                        wait(dve, rows_ready, t - G - AWAY + 1)
                        v.scalar_tensor_tensor(away[:, t % AWAY, :], rank[:, g, :], s["goal"][:, g:g + 1], m[:, g, :],
                                               ALU.is_equal, ALU.mult).then_inc(aways, 1)
                    if g >= 1 and b >= 1:
                        dve.wait_ge(aways, t)
                        gone = away[:, (t - 1) % AWAY, :]
                        if b >= 2:
                            v.tensor_tensor(gone[:, 0:lo - P], gone[:, 0:lo - P], removed_in[b % 2][:, g - 1, 0:lo - P],
                                            ALU.add).then_inc(joined, 1)
                        v.tensor_tensor(gone[:, lo - P:lo], gone[:, lo - P:lo], cols_out[:, b, g - 1, :],
                                        ALU.add).then_inc(joined, 1)
                if b % 2 == 0:
                    dve.wait_ge(roots, h + 1)
                    then(v.tensor_scalar(dinv[:, h, :], dinv[:, h, :], 1e-6, None, ALU.add))
                    v.reciprocal(dinv[:, h, :], dinv[:, h, :]).then_inc(dinv_ready, 1)
                if b + 1 < NB:
                    static_part(b + 1)
            keep_own_cols(NB - 1)


def passes(nc, adj_t, params, keep_dram, u_dram, maskv, x1_dram, r_dram, out):
    G, N, _ = adj_t.shape
    NB = N // P
    NQ = N // 512
    RING = 6
    KRING = 8
    PASSES = 3
    DVE_DEG = (1, 4, 7, 10, 13)
    LAST = PASSES * G
    with ExitStack() as ctx:
        def sb(name, shape, dt=F32):
            return ctx.enter_context(nc.sbuf_tensor(name, shape, dt))

        def sem(name):
            return ctx.enter_context(nc.semaphore(name))

        ring = sb("ring", [P, RING, N])
        keep = sb("keep", [P, KRING, N], U8)
        y = sb("y", [P, G, NB, P])
        hbuf = [sb(f"hbuf{i}", [P, NB, P]) for i in range(2)]
        h_t = [sb(f"h_t{i}", [P, NB, P]) for i in range(2)]
        agg_t = sb("agg_t2", [P, N])
        obuf = sb("obuf", [P, NB, P])
        spare = sb("spare", [P, N])
        deg_pool = spare
        deg_dve = y[:, G - 1].rearrange("p a c -> p (a c)")
        x1_buf = spare[:].rearrange("p (a c) -> p a c", c=P)
        w = sb("w", [P, 19, P])
        ident = sb("identf", [P, P])
        ones = sb("ones_f", [P, P])
        sums = sb("sums", [P, 2, 512])
        gain = sb("gain", [P, P])
        shift = sb("shift", [P, P])
        mean = sb("mean", [P, P])
        var = sb("var", [P, P])
        gain_col = sb("gain_col", [P, 1])
        shift_col = sb("shift_col", [P, 1])
        deg_inv = sb("deg_inv", [P, G, NB])
        mask2 = sb("mask2", [P, NB, G])
        ln_neg_mean = sb("ln_neg_mean", [P, NB])
        ln_var = sb("ln_var", [P, NB])
        ln_scale = sb("ln_scale", [P, NB])
        ln_bias = sb("ln_bias", [P, NB])
        squares = sb("squares", [P, NB])
        norm = sb("norm", [P, NB])
        acc = [ctx.enter_context(nc.psum_tensor(f"acc2{i}", [P, 512], F32)) for i in range(NQ)]
        pe_a = [ctx.enter_context(nc.psum_tensor(f"pe_a{i}", [P, 512], F32)) for i in range(2)]
        pe_x = [ctx.enter_context(nc.psum_tensor(f"pe_x{i}", [P, 512], F32)) for i in range(2)]
        bias_row = [w[:, i, :] for i in (2, 5, 8)]
        gains = [w[:, i, :] for i in (9, 15, 17)]
        shifts = [w[:, i, :] for i in (10, 16, 18)]
        bl = w[:, 11, :]

        consts = sem("c_consts")
        params_in = sem("c_params_in")
        h_in = [sem(f"h_in{i}") for i in range(2)]
        tile_in = [sem(f"c_tile_in{i}") for i in range(RING)]
        keep_in = [sem(f"keep_in{i}") for i in range(KRING)]
        masked = sem("masked")
        deg_added_pool = sem("deg_added_pool")
        deg_added_dve = sem("deg_added_dve")
        deg_done = sem("deg_done")
        deg_read = sem("deg_read")
        step = sem("c_step")
        pool_step = sem("c_pool_step")
        act_step = sem("c_act_step")
        summed = sem("summed")
        bn_var = sem("bn_var")
        bn_root = sem("bn_root")
        bn_ready = sem("bn_ready")
        bn_turned = sem("bn_turned")
        bn_cols = sem("bn_cols")
        ln_mean_ready = sem("ln_mean_ready")
        ln_squared = sem("ln_squared")
        ln_var_ready = sem("ln_var_ready")
        ln_root = sem("ln_root")
        ln_scale_ready = sem("ln_scale_ready")
        ln_done = sem("ln_done")
        x1_stored = [sem(f"x1_stored{i}") for i in range(2)]
        x1_in = sem("x1_in")
        x1_added = sem("x1_added")
        h_ready = sem("h_ready")
        h_turned = sem("h_turned")
        h_t_ready = sem("h_t_ready")
        y_done = sem("y_done")
        y_read = sem("y_read")
        tile_used = sem("c_tile_used")
        agg_ready = sem("c_agg_ready")
        out_done = sem("out_done")
        out_read = sem("out_read")
        out_ready = sem("out_ready")
        norm_root = sem("norm_root")
        norm_ready = sem("norm_ready")
        r_ready = sem("r_ready")
        r_squared = sem("r_squared")
        r_summed = sem("r_summed")
        r_stored = sem("r_stored")
        out_stored = sem("out_stored")
        block = ctx.enter_context(nc.Block())

        def wait(eng, s, value):
            if value > 0:
                eng.wait_ge(s, value)

        def deg_count(t, by_dve):
            return sum((i % NB in DVE_DEG) == by_dve for i in range(min(t, G * NB)))

        def tile(t):
            return ring[:, t % RING, :]

        @block.sync
        def _(sp):
            sp.dma_start(w[:], params[:, 1:20, :]).then_inc(params_in, 16)

            def load_h(n):
                wait(sp, tile_used, min(n - 1, LAST) * NB)
                wait(sp, h_turned, (n - 1) * NQ)
                if n >= 2:
                    sp.wait_ge(x1_stored[n % 2], 16 * min(n // 2, G // 2))
                if n >= G:
                    sp.wait_ge(r_stored, 16 * (n - G + 1))
                src = u_dram if n < G else r_dram
                sp.dma_start(hbuf[n % 2][:], src[n % G]).then_inc(h_in[n % 2], 16)

            load_h(0)
            for n in range(LAST):
                g = n % G
                for j in range(NB):
                    t = n * NB + j
                    rows = slice(j * P, (j + 1) * P)
                    wait(sp, tile_used, t - RING + 1)
                    wait(sp, deg_added_pool, deg_count(t - RING + 1, False))
                    wait(sp, deg_added_dve, deg_count(t - RING + 1, True))
                    sp.dma_start(tile(t), adj_t[g, rows, :]).then_inc(tile_in[t % RING], 16)
                    wait(sp, masked, t - KRING + 1)
                    sp.dma_start(keep[:, t % KRING, :], keep_dram[g, rows, :]).then_inc(keep_in[t % KRING], 16)
                    if j == 1:
                        load_h(n + 1)
                        if n >= 2 * G:
                            wait(sp, x1_added, g)
                            if g == 0:
                                for i in range(2):
                                    sp.wait_ge(x1_stored[i], 16 * G // 2)
                            sp.dma_start(x1_buf, x1_dram[g]).then_inc(x1_in, 16)
            for g in range(1, G):
                load_h(LAST + g)

        @block.gpsimd
        def _(pool):
            nc.gpsimd.memset(ident[:], 0.0).then_inc(consts, 1)
            nc.gpsimd.memset(ones[:], 1.0).then_inc(consts, 1)
            pool.wait_ge(consts, 2)
            nc.gpsimd.affine_select(out=ident[:], in_=ident[:], compare_op=ALU.not_equal, fill=1.0, base=0,
                                    pattern=[[-1, P]], channel_multiplier=1).then_inc(consts, 1)
            steps = [0]

            def then(ins):
                steps[0] += 1
                ins.then_inc(pool_step, 1)
                pool.wait_ge(pool_step, steps[0])

            def add_sums(n, q):
                if q == 0:
                    pool.wait_ge(r_ready, (n + 1) * NB)
                    pool.wait_ge(r_squared, n + 1)
                cols = slice(512 * q, 512 * q + 512)
                r = obuf[:, 4 * q:4 * q + 4, :].rearrange("p a c -> p (a c)")
                nc.gpsimd.tensor_tensor(sums[:, 0, :], sums[:, 0, :], r, ALU.add).then_inc(r_summed, 1)
                nc.gpsimd.tensor_tensor(sums[:, 1, :], sums[:, 1, :], agg_t[:, cols], ALU.add).then_inc(r_summed, 1)
                pool.wait_ge(r_summed, 2 * (n * NQ + q + 1))

            for n in range(LAST):
                p, g = divmod(n, G)
                if g == 0:
                    wait(pool, summed, p)
                    then(nc.gpsimd.memset(sums[:], 0.0))
                for j in range(NB):
                    t = n * NB + j
                    if p == 0 and j not in DVE_DEG:
                        pool.wait_ge(masked, t + 1)
                        if j == 0:
                            wait(pool, deg_done, n)
                            nc.gpsimd.tensor_copy(deg_pool[:], tile(t)).then_inc(deg_added_pool, 1)
                        else:
                            pool.wait_ge(deg_added_pool, deg_count(t, False))
                            nc.gpsimd.tensor_tensor(deg_pool[:], deg_pool[:], tile(t), ALU.add).then_inc(deg_added_pool, 1)
                    if g > 0 and 8 <= j < 8 + NQ:
                        add_sums(n - 1, j - 8)
                if g == G - 1:
                    for q in range(NQ):
                        add_sums(n, q)

        @block.scalar
        def _(act):
            steps = [0]

            def turn(n):
                for q in range(NQ):
                    act.wait_ge(h_turned, n * NQ + q + 1)
                    if q == 0 and n >= 2:
                        act.wait_ge(out_done, min(n - 1, LAST) * NQ)
                        wait(act, y_done, (n - 1 - G) * NQ)
                    src = rows4(pe_a[q % 2])
                    dst = h_t[n % 2][:, 4 * q:4 * q + 4, :]
                    if n < LAST:
                        nc.scalar.activation(dst, src, ACT.Copy).then_inc(h_t_ready, 1)
                    else:
                        nc.scalar.activation(dst, src, ACT.Identity, scale=gain_col[:], bias=shift_col[:]).then_inc(h_t_ready, 1)

            def ln_squares(k, src, junk):
                act.wait_ge(ln_mean_ready, k + 1)
                for i in range(NB):
                    nc.scalar.activation(junk[:, i, :], src[:, i, :], ACT.Square, bias=ln_neg_mean[:, i:i + 1],
                                         accum_out=ln_var[:, i:i + 1]).then_inc(ln_squared, 1)
                act.wait_ge(ln_var_ready, k + 1)
                nc.scalar.activation(ln_scale[:], ln_var[:], ACT.Sqrt).then_inc(ln_root, 1)

            def ln_apply(k, buf):
                act.wait_ge(ln_scale_ready, k + 1)
                for i in range(NB):
                    nc.scalar.activation(buf[:, i, :], buf[:, i, :], ACT.Identity, scale=ln_scale[:, i:i + 1],
                                         bias=ln_bias[:, i:i + 1]).then_inc(ln_done, 1)

            def x1(n):
                act.wait_ge(h_in[n % 2], 16 * (n // 2 + 1))
                wait(act, out_done, (n - 1) * NQ)
                ln_squares(n, hbuf[n % 2], h_t[n % 2])
                ln_apply(n, hbuf[n % 2])
                act.wait_ge(ln_done, (n + 1) * NB)
                act.dma_start(x1_dram[n], hbuf[n % 2][:]).then_inc(x1_stored[n % 2], 16)

            def norm_squares(n):
                act.wait_ge(out_ready, n + 1)
                act.wait_ge(out_done, (n + 1) * NQ)
                for i in range(NB):
                    nc.scalar.activation(agg_t[:, i * P:(i + 1) * P], obuf[:, i, :], ACT.Square,
                                         accum_out=squares[:, i:i + 1]).then_inc(act_step, 1)
                steps[0] += NB
                act.wait_ge(act_step, steps[0])
                nc.scalar.activation(norm[:], squares[:], ACT.Sqrt).then_inc(norm_root, 1)

            def norm_apply(n):
                act.wait_ge(norm_ready, n + 1)
                for i in range(NB):
                    nc.scalar.activation(obuf[:, i, :], obuf[:, i, :], ACT.Relu, scale=norm[:, i:i + 1]).then_inc(r_ready, 1)
                act.wait_ge(r_ready, (n + 1) * NB)
                act.dma_start(r_dram[n % G], obuf[:]).then_inc(r_stored, 16)
                nc.scalar.activation(agg_t[:], obuf[:].rearrange("p a c -> p (a c)"), ACT.Square).then_inc(r_squared, 1)

            def bn(p):
                act.wait_ge(bn_var, p)
                nc.scalar.activation(var[:], var[:], ACT.Sqrt).then_inc(bn_root, 1)

            x1(0)
            turn(0)
            for n in range(LAST):
                p, g = divmod(n, G)
                if g == 0 and p > 0:
                    bn(p)
                    turn(n)
                if g > 0:
                    norm_apply(n - 1)
                if p == 0 and g + 1 < G:
                    x1(n + 1)
                act.wait_ge(tile_used, (n + 1) * NB)
                wait(act, r_summed, 2 * n * NQ)
                for q in range(NQ):
                    nc.scalar.activation(agg_t[:, 512 * q:512 * q + 512], acc[q][:], ACT.Copy).then_inc(agg_ready, 1)
                if g + 1 < G:
                    turn(n + 1)
                norm_squares(n)
                if g == G - 1:
                    norm_apply(n)
            bn(PASSES)
            act.wait_ge(bn_cols, 1)
            act.wait_ge(r_summed, 2 * LAST * NQ)
            agg_blocks = agg_t[:].rearrange("p (a c) -> p a c", c=P)

            def finish(g):
                ln_apply(G + g, y[:, g])
                act.wait_ge(ln_done, (G + g + 1) * NB)
                act.dma_start(out[g], y[:, g]).then_inc(out_stored, 16)

            turn(LAST)
            for g in range(G):
                if g + 1 < G:
                    turn(LAST + g + 1)
                ln_squares(G + g, y[:, g], agg_blocks)
                finish(g)
            act.wait_ge(r_stored, 16 * LAST)
            for i in range(2):
                act.wait_ge(x1_stored[i], 16 * G // 2)
            act.wait_ge(out_stored, 16 * G)

        @block.tensor
        def _(pe):
            pe.wait_ge(consts, 3)
            pe.wait_ge(params_in, 16)

            def batch_sums(p):
                pe.wait_ge(r_summed, 2 * p * G * NQ)
                pe.wait_ge(out_read, p * G * NQ)
                for i in range(2):
                    for a in range(4):
                        mm = pe.matmul(pe_x[0][:, i * P:(i + 1) * P], ones[:], sums[:, i, a * P:(a + 1) * P],
                                       start=(a == 0), stop=(a == 3))
                mm.then_inc(summed, 1)

            def turn_h(n):
                if n < G:
                    pe.wait_ge(ln_done, (n + 1) * NB)
                elif n < LAST:
                    pe.wait_ge(h_ready, n - G + 1)
                else:
                    pe.wait_ge(h_in[n % 2], 16 * (n // 2 + 1))
                for q in range(NQ):
                    wait(pe, h_t_ready, n * NQ + q - 1)
                    wait(pe, out_read, min(n if n % G == 0 else n - 1, LAST) * NQ)
                    for a in range(4):
                        mm = pe.transpose(pe_a[q % 2][:, a * P:(a + 1) * P], hbuf[n % 2][:, 4 * q + a, :], ident[:])
                    mm.then_inc(h_turned, 1)

            def wl_share(n):
                wl = w[:, 12 + n // G - 1, :]
                m = n - G
                for q in range(NQ):
                    pe.wait_ge(h_t_ready, n * NQ + q + 1)
                    wait(pe, y_read, m * NQ + q - 1)
                    for a in range(4):
                        mm = pe.matmul(pe_x[q % 2][:, a * P:(a + 1) * P], h_t[n % 2][:, 4 * q + a, :], wl, start=True, stop=True)
                    mm.then_inc(y_done, 1)

            turn_h(0)
            for n in range(LAST):
                p, g = divmod(n, G)
                wr, wx = w[:, 3 * p, :], w[:, 3 * p + 1, :]
                if g == 0 and p > 0:
                    batch_sums(p)
                    turn_h(n)
                    wl_share(n)
                wait(pe, agg_ready, n * NQ)
                for j in range(NB):
                    t = n * NB + j
                    pe.wait_ge(masked, t + 1)
                    for q in range(NQ):
                        mm = pe.matmul(acc[q][:], hbuf[n % 2][:, j, :], ring[:, t % RING, 512 * q:512 * q + 512],
                                       start=(j == 0), stop=(j == NB - 1))
                    mm.then_inc(tile_used, 1)
                if g + 1 < G:
                    turn_h(n + 1)
                    if p > 0:
                        wl_share(n + 1)
                if p == 0:
                    pe.wait_ge(deg_added_pool, deg_count((n + 1) * NB, False))
                    pe.wait_ge(deg_added_dve, deg_count((n + 1) * NB, True))
                    wait(pe, out_read, n * NQ)
                    for i in range(NB):
                        pe.matmul(pe_x[0][:, i:i + 1], deg_pool[:, i * P:(i + 1) * P], ones[:, 0:1], start=True, stop=False)
                        mm = pe.matmul(pe_x[0][:, i:i + 1], deg_dve[:, i * P:(i + 1) * P], ones[:, 0:1], start=False, stop=True)
                    mm.then_inc(deg_done, 1)
                    pe.wait_ge(deg_read, n + 1)
                ahead = n + 2 if g + 1 < G else n + 1
                pe.wait_ge(h_t_ready, ahead * NQ)
                wait(pe, y_read, (ahead - G) * NQ)
                for q in range(NQ):
                    pe.wait_ge(agg_ready, n * NQ + q + 1)
                    wait(pe, out_read, n * NQ + q - 1)
                    for a in range(4):
                        i = 4 * q + a
                        cols = slice(a * P, (a + 1) * P)
                        pe.matmul(pe_a[q % 2][:, cols], agg_t[:, i * P:(i + 1) * P], wr, start=True, stop=True)
                        mm = pe.matmul(pe_x[q % 2][:, cols], h_t[n % 2][:, i, :], wx, start=True, stop=True)
                    mm.then_inc(out_done, 1)
            batch_sums(PASSES)
            pe.wait_ge(bn_ready, PASSES)
            pe.transpose(pe_x[1][:, 0:P], gain[:], ident[:])
            pe.transpose(pe_x[1][:, P:2 * P], shift[:], ident[:]).then_inc(bn_turned, 1)
            pe.wait_ge(bn_cols, 1)
            turn_h(LAST)
            for g in range(G):
                wl_share(LAST + g)
                if g + 1 < G:
                    turn_h(LAST + g + 1)

        @block.vector
        def _(dve):
            v = nc.vector
            steps = [0]

            def then(ins):
                steps[0] += 1
                ins.then_inc(step, 1)
                dve.wait_ge(step, steps[0])

            done = [0]

            def mask_until(t_end):
                for t in range(done[0], min(t_end, LAST * NB)):
                    done[0] += 1
                    dve.wait_ge(keep_in[t % KRING], 16 * (t // KRING + 1))
                    dve.wait_ge(tile_in[t % RING], 16 * (t // RING + 1))
                    v.scalar_tensor_tensor(tile(t), tile(t), 0.0, keep[:, t % KRING, :], ALU.max, ALU.mult).then_inc(masked, 1)
                    if t < G * NB and t % NB in DVE_DEG:
                        dve.wait_ge(masked, t + 1)
                        if t % NB == DVE_DEG[0]:
                            wait(dve, deg_done, t // NB)
                            v.tensor_copy(deg_dve, tile(t)).then_inc(deg_added_dve, 1)
                        else:
                            dve.wait_ge(deg_added_dve, deg_count(t, True))
                            v.tensor_tensor(deg_dve, deg_dve, tile(t), ALU.add).then_inc(deg_added_dve, 1)

            def ln_mean(k, src):
                wait(dve, ln_done, k * NB)
                then(v.tensor_reduce(ln_neg_mean[:], src, AX.X, ALU.add))
                v.tensor_scalar(ln_neg_mean[:], ln_neg_mean[:], -1.0 / P, None, ALU.mult).then_inc(ln_mean_ready, 1)

            def ln_variance(k):
                dve.wait_ge(ln_squared, (k + 1) * NB)
                v.tensor_scalar(ln_var[:], ln_var[:], 1.0 / P, 1e-5, ALU.mult, ALU.add).then_inc(ln_var_ready, 1)

            def ln_scales(k):
                dve.wait_ge(ln_root, k + 1)
                then(v.reciprocal(ln_scale[:], ln_scale[:]))
                v.tensor_tensor(ln_bias[:], ln_neg_mean[:], ln_scale[:], ALU.mult).then_inc(ln_scale_ready, 1)

            def batch_norm(p):
                M = 1.0 / (G * N)
                dve.wait_ge(summed, p)
                then(v.tensor_scalar(mean[:], pe_x[0][:, 0:P], M, None, ALU.mult))
                then(v.tensor_tensor(gain[:], mean[:], mean[:], ALU.mult))
                then(v.scalar_tensor_tensor(var[:], pe_x[0][:, P:2 * P], M, gain[:], ALU.mult, ALU.subtract))
                then(v.tensor_scalar(var[:], var[:], 0.0, None, ALU.max))
                v.tensor_scalar(var[:], var[:], 1e-5, None, ALU.add).then_inc(bn_var, 1)
                dve.wait_ge(bn_root, p)
                then(v.reciprocal(gain[:], var[:]))
                then(v.tensor_tensor(gain[:], gain[:], gains[p - 1], ALU.mult))
                then(v.tensor_tensor(shift[:], mean[:], gain[:], ALU.mult))
                v.tensor_tensor(shift[:], shifts[p - 1], shift[:], ALU.subtract).then_inc(bn_ready, 1)
                dve.wait_ge(bn_ready, p)

            def normalize(n):
                dve.wait_ge(h_in[n % 2], 16 * (n // 2 + 1))
                h = hbuf[n % 2]
                then(v.tensor_tensor(h[:], h[:], over_blocks(gain[:], NB), ALU.mult))
                v.tensor_tensor(h[:], h[:], over_blocks(shift[:], NB), ALU.add).then_inc(h_ready, 1)

            def add_y(n):
                p, g = divmod(n, G)
                m = n - G
                for q in range(NQ):
                    dve.wait_ge(y_done, m * NQ + q + 1)
                    yq = y[:, g, 4 * q:4 * q + 4, :]
                    if p == 1:
                        v.tensor_copy(yq, rows4(pe_x[q % 2])).then_inc(y_read, 1)
                    else:
                        v.tensor_tensor(yq, yq, rows4(pe_x[q % 2]), ALU.add).then_inc(y_read, 1)

            def add_x1(n):
                g = n % G
                yg = y[:, g]
                dve.wait_ge(y_read, (n - G + 1) * NQ)
                then(v.tensor_tensor(yg, yg, over_columns(maskv[:, :, g], NB), ALU.mult))
                then(v.tensor_tensor(yg, yg, over_blocks(bl, NB), ALU.add))
                then(v.tensor_tensor(yg, yg, over_columns(maskv[:, :, g], NB), ALU.mult))
                dve.wait_ge(x1_in, 16 * (g + 1))
                v.tensor_tensor(yg, yg, x1_buf, ALU.add).then_inc(x1_added, 1)

            def read_out(n):
                g = n % G
                wait(dve, r_stored, 16 * n)
                wait(dve, r_summed, 2 * n * NQ)
                wait(dve, r_squared, n)
                for q in range(NQ):
                    dve.wait_ge(out_done, n * NQ + q + 1)
                    o = obuf[:, 4 * q:4 * q + 4, :]
                    then(v.tensor_tensor(o, rows4(pe_a[q % 2]), over_columns(deg_inv[:, g, 4 * q:4 * q + 4], 4), ALU.mult))
                    v.tensor_tensor(o, o, rows4(pe_x[q % 2]), ALU.add).then_inc(out_read, 1)
                dve.wait_ge(out_read, (n + 1) * NQ)
                v.tensor_tensor(obuf[:], obuf[:], over_blocks(bias_row[n // G], NB), ALU.add).then_inc(out_ready, 1)

            def norm_scale(n):
                dve.wait_ge(norm_root, n + 1)
                then(v.tensor_scalar(norm[:], norm[:], 1e-12, None, ALU.max))
                then(v.reciprocal(norm[:], norm[:]))
                v.tensor_tensor(norm[:], norm[:], maskv[:, :, n % G], ALU.mult).then_inc(norm_ready, 1)

            def degree(n):
                dve.wait_ge(deg_done, n + 1)
                v.tensor_scalar(deg_inv[:, n, :], pe_x[0][:, 0:NB], 1.0, None, ALU.max).then_inc(deg_read, 1)
                dve.wait_ge(deg_read, n + 1)
                then(v.reciprocal(deg_inv[:, n, :], deg_inv[:, n, :]))

            dve.wait_ge(params_in, 16)
            then(v.tensor_tensor(mask2[:], maskv[:], maskv[:], ALU.mult))
            dve.wait_ge(h_in[0], 16)
            ln_mean(0, hbuf[0][:])
            mask_until(1)
            ln_variance(0)
            mask_until(2)
            ln_scales(0)
            for n in range(LAST):
                p, g = divmod(n, G)
                first = n * NB
                if g == 0 and p > 0:
                    batch_norm(p)
                    normalize(n)
                    add_y(n)
                mask_until(first + 5)
                if g > 0:
                    norm_scale(n - 1)
                mask_until(first + 7)
                if g + 1 < G:
                    if p == 0:
                        dve.wait_ge(h_in[(n + 1) % 2], 16 * ((n + 1) // 2 + 1))
                        ln_mean(n + 1, hbuf[(n + 1) % 2][:])
                        mask_until(first + 10)
                        ln_variance(n + 1)
                        mask_until(first + 11)
                        ln_scales(n + 1)
                    else:
                        normalize(n + 1)
                mask_until(first + 12)
                if p == PASSES - 1:
                    add_x1(n)
                mask_until(first + NB + 2)
                if p == 0:
                    degree(n)
                if g + 1 < G and p > 0:
                    add_y(n + 1)
                read_out(n)
                if g == G - 1:
                    norm_scale(n)
            batch_norm(PASSES)
            dve.wait_ge(bn_turned, 1)
            then(v.tensor_copy(gain_col[:], pe_x[1][:, 0:1]))
            v.tensor_copy(shift_col[:], pe_x[1][:, P:P + 1]).then_inc(bn_cols, 1)
            dve.wait_ge(x1_added, G)
            dve.wait_ge(r_stored, 16 * LAST)

            def add_last(g):
                n = LAST + g
                m = n - G
                for q in range(NQ):
                    dve.wait_ge(y_done, m * NQ + q + 1)
                    o = obuf[:, 4 * q:4 * q + 4, :]
                    yq = y[:, g, 4 * q:4 * q + 4, :]
                    v.tensor_tensor(o, rows4(pe_x[q % 2]), over_columns(mask2[:, 4 * q:4 * q + 4, g], 4), ALU.mult).then_inc(y_read, 1)
                    dve.wait_ge(y_read, m * NQ + q + 1)
                    then(v.tensor_tensor(yq, yq, o, ALU.add))

            add_last(0)
            for g in range(G):
                ln_mean(G + g, y[:, g])
                if g + 1 < G:
                    add_last(g + 1)
                ln_variance(G + g)
                ln_scales(G + g)


def program(nc, adj, adj_t, mask, x, x_diag, params, out):
    G, N, _ = adj.shape
    NB = N // P

    def scratch(name, shape, dt):
        return nc.dram_tensor(name, shape, dt).ap()

    keep_dram = scratch("keep_dram", (G, N, N), U8)
    removed_cols = scratch("removed_cols", (G, N, N), U8)
    u_dram = scratch("u_dram", (G, P, NB, P), F32)
    x1_dram = scratch("x1_dram", (G, P, NB, P), F32)
    r_dram = scratch("r_dram", (G, P, NB, P), F32)
    with ExitStack() as ctx:
        maskv = ctx.enter_context(nc.sbuf_tensor("maskv", [P, NB, G], F32))
        dilate(nc, adj, adj_t, mask, x, x_diag, params, keep_dram, removed_cols, u_dram, maskv)
        passes(nc, adj_t, params, keep_dram, u_dram, maskv, x1_dram, r_dram, out)


def kernel(**inputs):
    import numpy as _np
    import concourse.bacc as _bacc
    from concourse import mybir as _mybir
    from concourse.bass_utils import run_bass_kernel_spmd as _run

    adj, x, mask = (_np.asarray(inputs[n]) for n in ("adj", "x", "nodemask"))
    G, N, D = x.shape
    NB = N // P

    def weight(name):
        return _np.asarray(inputs[name]).reshape(-1, P, D)

    def spread(name):
        return _np.broadcast_to(_np.asarray(inputs["L1_gnn_" + name]), (1, P, D))

    params = _np.concatenate(
        [weight("L0_gnn_kernel"), weight("L1_gnn_Wr1"), weight("L1_gnn_Wx1"), spread("b1"),
         weight("L1_gnn_Wr2"), weight("L1_gnn_Wx2"), spread("b2"), weight("L1_gnn_Wr3"), weight("L1_gnn_Wx3"),
         spread("b3"), spread("g1"), spread("be1"), spread("bl"), weight("L1_gnn_Wl"),
         spread("g2"), spread("be2"), spread("g3"), spread("be3")]).transpose(1, 0, 2)
    laid_out = {
        "adj": adj,
        "adj_t": adj.transpose(0, 2, 1),
        "mask": mask.reshape(G, NB, P).transpose(2, 1, 0),
        "x": x.reshape(G, NB, P, D).transpose(0, 2, 1, 3),
        "x_diag": _np.diagonal(adj, axis1=1, axis2=2).reshape(G, NB, P).transpose(2, 0, 1),
        "params": params,
    }
    nc = _bacc.Bacc("TRN2", target_bir_lowering=False, num_devices=1)
    arrays, args = {}, []
    for name, a in laid_out.items():
        a = _np.ascontiguousarray(a)
        arrays[f"in_{name}_dram"] = a
        args.append(nc.dram_tensor(f"in_{name}_dram", a.shape, _mybir.dt.from_np(a.dtype), kind="ExternalInput").ap())
    args.append(nc.dram_tensor("out_dram", (G, P, NB, D), F32, kind="ExternalOutput").ap())
    program(nc, *args)
    r = _run(nc, [arrays], core_ids=[0])
    return r.results[0]["out_dram"].transpose(0, 2, 1, 3).reshape(G, N, D)
```

```python
import concourse.bass as bass
from concourse import mybir
from contextlib import ExitStack

ALU = mybir.AluOpType
ACT = mybir.ActivationFunctionType
AX = mybir.AxisListType
F32 = mybir.dt.float32
F16 = mybir.dt.float16
U8 = mybir.dt.uint8
I8 = mybir.dt.int8
I32 = mybir.dt.int32

P = 128
ROUND2 = 1.5 * 2.0 ** 24
CODE = 8192.0


def row(buf, gp, q, lo, hi):
    return buf[:, bass.ds(gp * 2 + q, 1), lo:hi].rearrange("p a c -> p (a c)")


def rows4(t):
    return t[:].rearrange("p (a c) -> p a c", a=4)


def over_columns(t, n, width=P):
    return t.rearrange("p (g o) -> p g o", o=1).broadcast_to([P, n, width])


def over_blocks(t, n):
    return t.rearrange("p (o c) -> p o c", o=1).broadcast_to([P, n, t.shape[1]])


def dilate(nc, adj, adj_t, mask, x, x_diag, params, keep, removed_cols, u_dram, maskv):
    G, N, _ = adj.shape
    NB = N // P
    NQ = N // 512
    HB = NB // 2
    RING = 3
    TRING = 3
    assert G == N // P // 2
    AWAY = 3
    LAG = 2
    with ExitStack() as ctx:
        def sb(name, shape, dt):
            return ctx.enter_context(nc.sbuf_tensor(name, shape, dt))

        def ps(name, shape, dt):
            return ctx.enter_context(nc.psum_tensor(name, shape, dt))

        def sem(name):
            return ctx.enter_context(nc.semaphore(name))

        adj_ring = sb("adj_ring", [P, RING, N], F32)
        member = [sb(f"member{i}", [P, G, N], I8) for i in range(2)]
        own = [sb(f"own{i}", [P, G, P], F16) for i in range(2)]
        rank = sb("rank", [P, G, N], F16)
        removed_in = [sb(f"removed_in{i}", [P, G, N - (3 - i) * P], U8) for i in range(2)]
        cols_out = sb("cols_out", [P, NB, G, P], U8)
        keep_own = sb("keep_own", [P, G, P], U8)
        away = sb("away", [P, AWAY, N], F16)
        keep_row = sb("keep_row", [P, 2, N - P], U8)
        ones = sb("ones", [P, 1], F16)
        ident = sb("ident", [P, P], F16)
        above = sb("above", [P, P], F16)
        maski = sb("maski", [P, NB, G], I32)
        maskf = sb("maskf", [P, NB, G], F32)
        code = sb("code", [P, G, P], F32)
        pairs = sb("pairs", [P, G, P], F16)
        hit_mid = sb("hit_mid", [P, G, P], F16)
        hit = sb("hit", [P, G, P], F16)
        own_gone = hit_mid
        s = {n: sb("s_" + n, [P, G], F32) for n in
             ("upper", "count0", "dm", "even", "big", "valid", "par", "t_mid", "t_low", "t_low0", "removed",
              "diff", "count", "odd", "x1", "x2", "x3", "half", "mid", "bias_lo", "bias_up", "goal", "scale", "sign", "fewer")}
        moved = sb("moved", [P, 1], F32)
        onesf = sb("onesf", [P, 1], F32)
        flag = sb("flag", [1, 1], I32)
        tile_ring = sb("tile_ring", [P, TRING, N], F32)
        xin = sb("xin", [P, NB, P], F32)
        ybuf = sb("ybuf", [P, NB, P], F32)
        w0 = sb("w0", [P, P], F32)
        diag = sb("diag", [P, G, NB], F32)
        adj_sum = sb("adj_sum", [P, G, NB], F32)
        dinv = sb("dinv", [P, G, NB], F32)

        turned = [ps(f"turned{i}", [P, HB, P], F16) for i in range(2)]
        turned_own = ps("turned_own", [P, G, P], F16)
        count_ps = ps("count_ps", [P, 512], F32)
        acc = [ps(f"acc{i}", [P, 512], F32) for i in range(NQ)]
        removed_ps = count_ps[:, 0:G]
        flag_ps = count_ps[0:1, 2 * G:2 * G + 1]

        consts = sem("consts")
        mask_in = sem("mask_in")
        params_in = sem("params_in")
        adj_in = [sem(f"adj_in{i}") for i in range(RING)]
        adj_read = sem("adj_read")
        own_ready = sem("own_ready")
        positive = sem("positive")
        removed_loaded = sem("removed_loaded")
        cols_stored = sem("cols_stored")
        joined = sem("joined")
        own_saved = sem("own_saved")
        own_kept = sem("own_kept")
        own_stored = sem("own_stored")
        rows_stored = [sem(f"rows_stored{i}") for i in range(2)]
        step = sem("step")
        pool_step = sem("pool_step")
        lower = sem("lower")
        own_turned = sem("own_turned")
        pairs_ready = sem("pairs_ready")
        in_round = sem("in_round")
        hits = sem("hits")
        counted = sem("counted")
        moved_ready = sem("moved_ready")
        flag_counted = sem("flag_counted")
        flag_ready = sem("flag_ready")
        hit_turned = sem("hit_turned")
        ranks = sem("ranks")
        dists = sem("dists")
        aways = sem("aways")
        rows_turned = sem("rows_turned")
        cols_ready = sem("cols_ready")
        rows_ready = sem("rows_ready")
        degrees = sem("degrees")
        roots = sem("roots")
        dinv_ready = sem("dinv_ready")
        x_in = sem("x_in")
        y_ready = sem("y_ready")
        tile_in = [sem(f"tile_in{i}") for i in range(TRING)]
        tile_ready = sem("tile_ready")
        tile_used = sem("tile_used")
        agg_ready = sem("agg_ready")
        w0_done = sem("w0_done")
        relu_ready = sem("relu_ready")
        u_ready = sem("u_ready")
        u_stored = sem("u_stored")

        def dist_count(t):
            return 2 * min(t, (NB - 1) * G) + max(0, t - (NB - 1) * G)

        def half_sums(u):
            return [("sum", u // 2, (u % 2) * HB + j) for j in range(HB)]

        reads = {(-1, 0): [("sign", 0, g) for g in range(G)]}
        for b in range(NB):
            reads[b, 0] = [("sign", b + 1, g) for g in range(G)] if b + 1 < NB else []
            if b == 0:
                reads[b, 0] += half_sums(0) + half_sums(1)
            reads[b, 1] = half_sums(b + 2) if b + 2 < NB else []
        first_read, n_read = {}, 0
        for key, tiles in reads.items():
            first_read[key] = n_read
            n_read += len(tiles)

        def sign_count(b, g):
            return first_read[b - 1, 0] + g + 1

        def agg_t(h):
            return tile_ring[:, (h + 1) * NB % TRING, :]

        def copies(b):
            cut = b + 1
            return [(i, lo, hi, kept) for i in range(2)
                    for lo, hi, kept in ((i * HB, min(cut, (i + 1) * HB), True), (max(cut, i * HB), (i + 1) * HB, False))
                    if lo < hi]

        def copied(t, half=0):
            b, g = divmod(t, G)
            return (G * sum(len(copies(i)) for i in range(b)) + (g * len(copies(b)) if g else 0)
                    + (sum(c[0] < half for c in copies(b)) if half else 0))

        def join_count(t):
            return max(0, min(t, 2 * G) - G) + 2 * max(0, t - 2 * G)

        def stores(b):
            return sum((i >= 1) + (i + 2 < NB) for i in range(b)) * G

        block = ctx.enter_context(nc.Block())

        def wait(eng, s, value):
            if value > 0:
                eng.wait_ge(s, value)

        @block.sync
        def _(sp):
            sp.dma_start(maski[:], mask).then_inc(mask_in, 16)

            def load_reads(key, some=slice(None)):
                for i, (kind, m, n) in list(enumerate(reads[key]))[some]:
                    t = first_read[key] + i
                    rows, g = (m, n) if kind == "sign" else (n, m)
                    wait(sp, adj_read, t - RING + 1)
                    sp.dma_start(adj_ring[:, t % RING, :], adj[g, rows * P:(rows + 1) * P, :]).then_inc(adj_in[t % RING], 16)

            load_reads((-1, 0))
            sp.dma_start(w0[:], params[:, 0, :]).then_inc(params_in, 16)
            sp.dma_start(diag[:], x_diag).then_inc(params_in, 16)
            for b in range(NB):
                if 1 <= b < NB - 1:
                    sp.wait_ge(cols_stored, 16 * stores(b))
                    wait(sp, joined, join_count(b * G))
                    sp.dma_start(removed_in[(b + 1) % 2][:, :, 0:b * P],
                                 removed_cols[:, (b + 1) * P:(b + 2) * P, 0:b * P].rearrange("g p c -> p g c")
                                 ).then_inc(removed_loaded, 16)
                load_reads((b, 0))
                if b % 2 == 0:
                    wait(sp, u_ready, b // 2)
                    sp.dma_start(xin[:], x[b // 2]).then_inc(x_in, 16)
                for j in range(HB):
                    t = b * HB + j
                    rows = (b % 2) * HB + j
                    wait(sp, tile_used, t - TRING + 1)
                    if rows == 0:
                        wait(sp, w0_done, b // 2 * NQ)
                    sp.dma_start(tile_ring[:, t % TRING, :], adj_t[b // 2, rows * P:(rows + 1) * P, :]).then_inc(tile_in[t % TRING], 16)
                    load_reads((b, 1), slice(j, j + 1))

        @block.gpsimd
        def _(pool):
            nc.gpsimd.memset(ident[:], 0.0).then_inc(consts, 1)
            nc.gpsimd.memset(above[:], 1.0).then_inc(consts, 1)
            nc.gpsimd.memset(ones[:], 1.0).then_inc(consts, 1)
            nc.gpsimd.memset(onesf[:], 1.0).then_inc(consts, 1)
            pool.wait_ge(consts, 4)
            nc.gpsimd.affine_select(out=ident[:], in_=ident[:], compare_op=ALU.not_equal, fill=1.0, base=0,
                                    pattern=[[-1, P]], channel_multiplier=1).then_inc(consts, 1)
            nc.gpsimd.affine_select(out=above[:], in_=above[:], compare_op=ALU.is_gt, fill=0.0, base=0,
                                    pattern=[[1, P]], channel_multiplier=-1).then_inc(consts, 1)

            def store_own(b):
                lo = b * P
                pool.wait_ge(own_kept, b + 1)
                pool.dma_start(keep[:, lo:lo + P, lo:lo + P].rearrange("g p c -> p g c"), keep_own[:]).then_inc(own_stored, 16)

            for b in range(NB):
                lo = b * P
                if b >= 1:
                    store_own(b - 1)
                for g in range(G):
                    t = b * G + g
                    pool.wait_ge(aways, t + 1)
                    nc.gpsimd.tensor_copy(own_gone[:, g, :], away[:, t % AWAY, lo:lo + P]).then_inc(own_saved, 1)
                    if b >= 1:
                        r = t - G
                        pool.wait_ge(joined, join_count(t + 1))
                        wait(pool, rows_stored[r % 2], 16 * (r // 2))
                        nc.gpsimd.tensor_scalar(keep_row[:, r % 2, 0:lo], away[:, t % AWAY, 0:lo], -1.0, 1.0,
                                                ALU.mult, ALU.add).then_inc(rows_ready, 1)
                        pool.wait_ge(rows_ready, r + 1)
                        pool.dma_start(keep[g, lo:lo + P, 0:lo], keep_row[:, r % 2, 0:lo]).then_inc(rows_stored[r % 2], 16)
                    if g == 0 and b % 2 == 0:
                        h = b // 2
                        pool.wait_ge(dinv_ready, h + 1)
                        pool.wait_ge(x_in, 16 * (h + 1))
                        wait(pool, u_stored, 16 * h)
                        nc.gpsimd.tensor_tensor(ybuf[:], xin[:], over_columns(dinv[:, h, :], NB), ALU.mult).then_inc(y_ready, 1)
                    t = b * HB + g
                    rows = (b % 2) * HB + g
                    pool.wait_ge(tile_in[t % TRING], 16 * (t // TRING + 1))
                    own_cols = tile_ring[:, t % TRING, rows * P:(rows + 1) * P]
                    nc.gpsimd.affine_select(out=own_cols, in_=own_cols, compare_op=ALU.not_equal, fill=1.0, base=0,
                                            pattern=[[-1, P]], channel_multiplier=1).then_inc(tile_ready, 1)
                h = b // 2
                if b % 2 == 1:
                    pool.wait_ge(relu_ready, (h + 1) * NB)
                    nc.gpsimd.tensor_tensor(ybuf[:], ybuf[:], xin[:], ALU.add).then_inc(u_ready, 1)
                    pool.wait_ge(u_ready, h + 1)
                    pool.dma_start(u_dram[h], ybuf[:]).then_inc(u_stored, 16)
            pool.wait_ge(u_stored, 16 * G)
            store_own(NB - 1)
            pool.wait_ge(own_stored, 16 * NB)
            for i in range(2):
                pool.wait_ge(rows_stored[i], 16 * G * (NB - 1) // 2)

        @block.scalar
        def _(act):
            positives = [0]

            def read(key, some=slice(None)):
                for i, (kind, m, n) in list(enumerate(reads[key]))[some]:
                    t = first_read[key] + i
                    tile = adj_ring[:, t % RING, :]
                    act.wait_ge(adj_in[t % RING], 16 * (t // RING + 1))
                    if kind == "sign":
                        if n == 0:
                            wait(act, aways, (m - 1) * G)
                        positives[0] += 1
                        nc.scalar.activation(tile, tile, ACT.Relu).then_inc(positive, 1)
                        act.wait_ge(positive, positives[0])
                        nc.scalar.activation(member[m % 2][:, n, :], tile, ACT.Sign).then_inc(adj_read, 1)
                    else:
                        nc.scalar.activation(tile, tile, ACT.Copy, accum_out=adj_sum[:, m, n:n + 1]).then_inc(adj_read, 1)

            read((-1, 0))
            for b in range(NB):
                read((b, 0))
                h = b // 2
                if b % 2 == 0:
                    act.wait_ge(degrees, h + 1)
                    nc.scalar.activation(dinv[:, h, :], dinv[:, h, :], ACT.Sqrt).then_inc(roots, 1)
                act.wait_ge(ranks, b + 1)
                W = (b + 1) * P
                for g in range(G + LAG):
                    if g < G:
                        nc.scalar.activation(rank[:, g, 0:W], rank[:, g, 0:W], ACT.Abs, bias=s["bias_lo"][:, g:g + 1],
                                             scale=s["scale"][:, g:g + 1]).then_inc(dists, 1)
                        if W < N:
                            nc.scalar.activation(rank[:, g, W:N], rank[:, g, W:N], ACT.Abs, bias=s["bias_up"][:, g:g + 1],
                                                 scale=s["scale"][:, g:g + 1]).then_inc(dists, 1)
                    if g >= LAG:
                        d = g - LAG
                        t = b * G + d
                        if d == 0 and b >= 1:
                            act.wait_ge(cols_stored, 16 * stores(b))
                            act.wait_ge(own_kept, b)
                        wait(act, joined, join_count(t + 1))
                        for i, first, end, kept in copies(b):
                            act.wait_ge(rows_turned, 2 * t + i + 1)
                            nc.scalar.activation(cols_out[:, first:end, d, :], turned[i][:, first - i * HB:end - i * HB, :],
                                                 ACT.Identity, scale=-1.0 if kept else 1.0,
                                                 bias=1.0 if kept else 0.0).then_inc(cols_ready, 1)
                        act.wait_ge(cols_ready, copied(t + 1))
                        if b >= 1:
                            act.dma_start(keep[d, 0:b * P, b * P:(b + 1) * P].rearrange("(j p) c -> p j c", p=P),
                                          cols_out[:, 0:b, d, :]).then_inc(cols_stored, 16)
                        if b + 2 < NB:
                            act.dma_start(removed_cols[d, (b + 2) * P:, b * P:(b + 1) * P].rearrange("(j p) c -> p j c", p=P),
                                          cols_out[:, b + 2:, d, :]).then_inc(cols_stored, 16)
                        read((b, 1), slice(d, d + 1))
                if b % 2 == 1:
                    act.wait_ge(tile_used, (b + 1) * HB)
                    for q in range(NQ):
                        nc.scalar.activation(agg_t(h)[:, 512 * q:512 * q + 512], acc[q][:], ACT.Copy).then_inc(agg_ready, 1)
                    for i in range(NB):
                        if i % 4 == 0:
                            act.wait_ge(w0_done, h * NQ + i // 4 + 1)
                        nc.scalar.activation(ybuf[:, i, :], acc[i // 4][:, (i % 4) * P:(i % 4 + 1) * P], ACT.Relu,
                                             scale=dinv[:, h, i:i + 1]).then_inc(relu_ready, 1)
            act.wait_ge(cols_stored, 16 * stores(NB))

        @block.tensor
        def _(pe):
            pe.wait_ge(consts, 6)
            pe.wait_ge(params_in, 32)
            rounds = pe.alloc_register("pe_rounds")
            pe.reg_mov(rounds, 0)
            still = pe.alloc_register("pe_still")

            def turn_own(b):
                pe.wait_ge(own_ready, b + 1)
                for g in range(G):
                    mm = pe.transpose(turned_own[:, g, :], own[b % 2][:, g, :], ident[:])
                mm.then_inc(own_turned, 1)

            turn_own(0)
            for b in range(NB):
                h = b // 2
                pe.reg_mov(still, 1)
                with pe.While(lambda: pe.snap(still) != 0):
                    done = pe.snap(rounds)
                    pe.wait_ge(hits, done + 1)
                    for g in range(G):
                        mm = pe.matmul(removed_ps[:, g:g + 1], hit[:, g, :], ones[:], start=True, stop=True)
                    mm.then_inc(counted, 1)
                    pe.wait_ge(moved_ready, done + 1)
                    pe.matmul(flag_ps, moved[:], onesf[:], start=True, stop=True).then_inc(flag_counted, 1)
                    pe.wait_ge(flag_ready, done + 1)
                    pe.reg_add(rounds, rounds, 1)
                    pe.reg_load(still, flag[0:1, 0:1])
                for g in range(G):
                    mm = pe.transpose(turned_own[:, g, :], hit[:, g, :], ident[:])
                mm.then_inc(hit_turned, 1)
                for g in range(G):
                    t = b * G + g
                    pe.wait_ge(aways, t + 1)
                    for i in range(2):
                        if t > 0:
                            pe.wait_ge(cols_ready, copied(t - 1, i + 1) if i == 0 else copied(t))
                        if b > i * HB:
                            pe.wait_ge(joined, join_count(t + 1))
                        for j in range(HB):
                            c = i * HB + j
                            mm = pe.transpose(turned[i][:, j, :], away[:, t % AWAY, c * P:(c + 1) * P], ident[:])
                        mm.then_inc(rows_turned, 1)
                    t = b * HB + g
                    rows = (b % 2) * HB + g
                    if g == 0:
                        pe.wait_ge(y_ready, h + 1)
                    pe.wait_ge(tile_ready, t + 1)
                    if rows == 0:
                        wait(pe, relu_ready, h * NB)
                    for q in range(NQ):
                        mm = pe.matmul(acc[q][:], ybuf[:, rows, :], tile_ring[:, t % TRING, 512 * q:512 * q + 512],
                                       start=(rows == 0), stop=(rows == NB - 1))
                    mm.then_inc(tile_used, 1)
                if b + 1 < NB:
                    turn_own(b + 1)
                if b % 2 == 1:
                    for q in range(NQ):
                        pe.wait_ge(agg_ready, h * NQ + q + 1)
                        for a in range(4):
                            i = 4 * q + a
                            mm = pe.matmul(acc[q][:, a * P:(a + 1) * P], agg_t(h)[:, i * P:(i + 1) * P], w0[:], start=True, stop=True)
                        mm.then_inc(w0_done, 1)

        @block.vector
        def _(dve):
            steps = [0]

            def then(ins):
                steps[0] += 1
                ins.then_inc(step, 1)
                dve.wait_ge(step, steps[0])

            def begin(ins):
                steps[0] += 1
                ins.then_inc(step, 1)

            v = nc.vector
            dve.wait_ge(mask_in, 16)
            then(v.tensor_scalar(maskf[:], maski[:], 0.0, None, ALU.not_equal))
            then(v.tensor_copy(maskv[:], maski[:]))
            dve.wait_ge(params_in, 32)
            then(v.tensor_scalar(diag[:], diag[:], -1.0, 1.0, ALU.mult, ALU.add))
            dve.wait_ge(consts, 6)
            rounds = dve.alloc_register("dve_rounds")
            dve.reg_mov(rounds, 0)
            still = dve.alloc_register("dve_still")

            def bc(t):
                return over_columns(t[:], G)

            def scan(g, cols, m, start):
                width = cols.stop - cols.start
                v.tensor_tensor_scan(rank[:, g, cols], ones[:].broadcast_to([P, width]), m[:, g, cols], start,
                                     ALU.mult, ALU.add).then_inc(step, 1)
                steps[0] += 1

            def own_cols(b):
                dve.wait_ge(adj_read, sign_count(b, G - 1))
                v.tensor_copy(own[b % 2][:], member[b % 2][:, :, b * P:(b + 1) * P]).then_inc(own_ready, 1)

            def take_out(b, g):
                if b >= 2:
                    before = slice(0, (b - 1) * P)
                    m = member[b % 2]
                    dve.wait_ge(removed_loaded, 16 * (b - 1))
                    v.tensor_tensor(m[:, g, before], m[:, g, before], removed_in[b % 2][:, g, before], ALU.is_gt).then_inc(lower, 1)

            def first_ranks(b, g):
                wait(dve, aways, (b - 1) * G + g + 1)
                scan(g, slice(b * P, N), member[b % 2], 0.0)
                if b >= 2:
                    dve.wait_ge(lower, (b - 2) * G + g + 1)
                    scan(g, slice(0, (b - 1) * P), member[b % 2], 0.0)

            def keep_own_cols(b):
                dve.wait_ge(cols_ready, copied((b + 1) * G))
                dve.wait_ge(own_saved, (b + 1) * G)
                wait(dve, own_stored, 16 * b)
                v.scalar_tensor_tensor(keep_own[:], own_gone[:], 0.0, cols_out[:, b, :, :], ALU.is_equal,
                                       ALU.mult).then_inc(own_kept, 1)

            own_cols(0)
            for g in range(G):
                first_ranks(0, g)
            for b in range(NB):
                lo = b * P
                m = member[b % 2]
                diag_cols = slice(lo, lo + P)
                dve.wait_ge(step, steps[0])
                if b >= 1:
                    last = slice(lo - P, lo)
                    dve.wait_ge(cols_ready, copied(b * G))
                    then(v.tensor_tensor(m[:, :, last], m[:, :, last], cols_out[:, b, :, :], ALU.is_gt))
                    for g in range(G):
                        scan(g, last, m, rank[:, g, lo - P - 1:lo - P] if b >= 2 else 0.0)
                    dve.wait_ge(step, steps[0])
                if b >= 1:
                    keep_own_cols(b - 1)
                then(v.tensor_copy(s["upper"][:], rank[:, :, N - 1:N].rearrange("p g o -> p (g o)")))
                if b >= 1:
                    then(v.tensor_tensor(s["count0"][:], s["upper"][:], rank[:, :, lo - 1:lo].rearrange("p g o -> p (g o)"), ALU.add))
                else:
                    then(v.tensor_copy(s["count0"][:], s["upper"][:]))
                then(v.tensor_tensor(code[:], rank[:, :, diag_cols], bc(s["upper"]), ALU.subtract))
                then(v.tensor_scalar(code[:], code[:], 2.0, CODE + 1.0, ALU.mult, ALU.add))
                dve.wait_ge(own_ready, b + 1)
                then(v.tensor_tensor(pairs[:], own[b % 2][:], over_blocks(above[:], G), ALU.mult))
                dve.wait_ge(own_turned, b + 1)
                then(v.tensor_tensor(pairs[:], pairs[:], turned_own[:], ALU.mult))
                then(v.tensor_tensor(code[:], code[:], pairs[:], ALU.mult))
                then(v.tensor_scalar(code[:], code[:], -1.0, None, ALU.add))
                then(v.memset(s["removed"][:], 0.0))
                dve.reg_mov(still, 1)
                with dve.While(lambda: dve.snap(still) != 0):
                    done = dve.snap(rounds)
                    K = 13
                    k = [0]

                    def start(ins):
                        k[0] += 1
                        ins.then_inc(in_round, 1)

                    def link(ins):
                        start(ins)
                        dve.wait_ge(in_round, done * K + k[0])

                    link(v.scalar_tensor_tensor(s["dm"][:], s["count0"][:], -0.5, s["removed"][:], ALU.add, ALU.subtract))
                    start(v.tensor_scalar(s["even"][:], s["dm"][:], ROUND2, -ROUND2, ALU.add, ALU.add))
                    start(v.tensor_scalar(s["big"][:], s["dm"][:], 10.0, None, ALU.is_ge))
                    link(v.scalar_tensor_tensor(s["valid"][:], s["dm"][:], 1.0, maskf[:, b, :], ALU.is_ge, ALU.mult))
                    start(v.scalar_tensor_tensor(s["par"][:], s["dm"][:], 9500.0, s["even"][:], ALU.add, ALU.subtract))
                    link(v.tensor_tensor(s["big"][:], s["big"][:], maskf[:, b, :], ALU.mult))
                    link(v.scalar_tensor_tensor(s["t_low0"][:], s["valid"][:], -9498.0, s["par"][:], ALU.mult, ALU.add))
                    start(v.scalar_tensor_tensor(s["t_mid"][:], s["big"][:], CODE, s["even"][:], ALU.mult, ALU.subtract))
                    link(v.scalar_tensor_tensor(s["t_low"][:], s["big"][:], 8190.5, s["t_low0"][:], ALU.mult, ALU.add))
                    start(v.tensor_tensor(hit_mid[:], code[:], bc(s["t_mid"]), ALU.is_equal))
                    link(v.tensor_tensor(hit[:], code[:], bc(s["t_low"]), ALU.is_ge))
                    v.tensor_tensor(hit[:], hit[:], hit_mid[:], ALU.add).then_inc(hits, 1)
                    dve.wait_ge(counted, done + 1)
                    link(v.tensor_tensor(s["diff"][:], removed_ps, s["removed"][:], ALU.not_equal))
                    link(v.tensor_copy(s["removed"][:], removed_ps))
                    v.tensor_reduce(moved[:], s["diff"][:], AX.X, ALU.add).then_inc(moved_ready, 1)
                    assert k[0] == K
                    dve.wait_ge(flag_counted, done + 1)
                    v.tensor_copy(flag[:], flag_ps).then_inc(flag_ready, 1)
                    dve.wait_ge(flag_ready, done + 1)
                    dve.reg_add(rounds, rounds, 1)
                    dve.reg_load(still, flag[0:1, 0:1])
                dve.wait_ge(hit_turned, b + 1)
                then(v.scalar_tensor_tensor(m[:, :, diag_cols], turned_own[:], 0.0, m[:, :, diag_cols], ALU.is_equal, ALU.mult))
                for g in range(G):
                    scan(g, diag_cols, m, rank[:, g, lo - 1:lo] if b >= 1 else 0.0)
                then(v.tensor_scalar(s["count"][:], s["dm"][:], 0.5, None, ALU.add))
                begin(v.tensor_tensor(s["odd"][:], s["count"][:], s["even"][:], ALU.subtract))
                begin(v.tensor_scalar(s["sign"][:], s["valid"][:], 2.0, -1.0, ALU.mult, ALU.add))
                then(v.tensor_tensor(s["fewer"][:], s["count"][:], s["upper"][:], ALU.subtract))
                begin(v.tensor_tensor(s["fewer"][:], s["fewer"][:], s["big"][:], ALU.mult))
                begin(v.tensor_tensor(s["x2"][:], s["count"][:], s["odd"][:], ALU.add))
                then(v.scalar_tensor_tensor(s["x1"][:], s["odd"][:], 0.0, s["count"][:], ALU.is_equal, ALU.mult))
                then(v.tensor_tensor(s["x1"][:], s["x1"][:], s["odd"][:], ALU.add))
                then(v.tensor_scalar(s["half"][:], s["x1"][:], 0.25, None, ALU.mult))
                then(v.scalar_tensor_tensor(s["mid"][:], s["x2"][:], 0.5, s["half"][:], ALU.mult, ALU.add))
                begin(v.scalar_tensor_tensor(s["x2"][:], s["half"][:], 1.0, s["big"][:], ALU.subtract, ALU.mult))
                then(v.scalar_tensor_tensor(s["x3"][:], s["mid"][:], 1.0, s["big"][:], ALU.add, ALU.mult))
                begin(v.tensor_tensor(s["goal"][:], s["x2"][:], s["sign"][:], ALU.add))
                then(v.tensor_scalar(s["bias_lo"][:], s["x3"][:], -1.0, 1.0, ALU.mult, ALU.add))
                then(v.tensor_tensor(s["bias_up"][:], s["bias_lo"][:], s["fewer"][:], ALU.add))
                v.tensor_copy(s["scale"][:], s["big"][:]).then_inc(ranks, 1)
                h = b // 2
                if b % 2 == 0:
                    dve.wait_ge(adj_read, first_read[max(b - 1, 0), int(b > 0)] + len(reads[max(b - 1, 0), int(b > 0)]))
                    v.tensor_tensor(dinv[:, h, :], adj_sum[:, h, :], diag[:, h, :], ALU.add).then_inc(degrees, 1)
                if b + 1 < NB:
                    own_cols(b + 1)
                for g in range(G):
                    t = b * G + g
                    dve.wait_ge(dists, dist_count(t + 1))
                    wait(dve, rows_turned, 2 * (t - AWAY + 1))
                    wait(dve, own_saved, t - AWAY + 1)
                    wait(dve, rows_ready, t - G - AWAY + 1)
                    gone = away[:, t % AWAY, :]
                    v.scalar_tensor_tensor(gone, rank[:, g, :], s["goal"][:, g:g + 1], m[:, g, :],
                                           ALU.is_equal, ALU.mult).then_inc(aways, 1)
                    if b + 1 < NB:
                        take_out(b + 1, g)
                    if b >= 1:
                        dve.wait_ge(aways, t + 1)
                        if b >= 2:
                            v.tensor_tensor(gone[:, 0:lo - P], gone[:, 0:lo - P], removed_in[b % 2][:, g, 0:lo - P],
                                            ALU.add).then_inc(joined, 1)
                        v.tensor_tensor(gone[:, lo - P:lo], gone[:, lo - P:lo], cols_out[:, b, g, :], ALU.add).then_inc(joined, 1)
                    if g == 0 and b % 2 == 0:
                        dve.wait_ge(roots, h + 1)
                        then(v.tensor_scalar(dinv[:, h, :], dinv[:, h, :], 1e-6, None, ALU.add))
                        v.reciprocal(dinv[:, h, :], dinv[:, h, :]).then_inc(dinv_ready, 1)
                    if b + 1 < NB:
                        first_ranks(b + 1, g)
            keep_own_cols(NB - 1)


def passes(nc, adj_t, params, keep_dram, u_dram, maskv, x1_dram, r_dram, out):
    G, N, _ = adj_t.shape
    NB = N // P
    NQ = N // 512
    RING = 7
    KRING = 6
    PASSES = 3
    DELAY = 2
    DVE_DEG = (1, 4, 7, 10, 13)
    LAST = PASSES * G
    with ExitStack() as ctx:
        def sb(name, shape, dt=F32):
            return ctx.enter_context(nc.sbuf_tensor(name, shape, dt))

        def sem(name):
            return ctx.enter_context(nc.semaphore(name))

        ring = sb("ring", [P, RING, N])
        keep = sb("keep", [P, KRING, N], U8)
        y = sb("y", [P, G, NB, P])
        hbuf = [sb(f"hbuf{i}", [P, NB, P]) for i in range(2)]
        h_t = [sb(f"h_t{i}", [P, NB, P]) for i in range(2)]
        agg_t = sb("agg_t2", [P, N])
        obuf = sb("obuf", [P, NB, P])
        x1_buf = sb("x1_buf", [P, NB, P])
        deg_pool = [y[:, i].rearrange("p a c -> p (a c)") for i in (0, 1)]
        deg_dve = [y[:, i].rearrange("p a c -> p (a c)") for i in (2, 3)]
        w = sb("w", [P, 19, P])
        ident = sb("identf", [P, P])
        ones = sb("ones_f", [P, P])
        sums = sb("sums", [P, 2, 512])
        gain = sb("gain", [P, P])
        shift = sb("shift", [P, P])
        mean = sb("mean", [P, P])
        var = sb("var", [P, P])
        gain_col = sb("gain_col", [P, 1])
        shift_col = sb("shift_col", [P, 1])
        deg_inv = sb("deg_inv", [P, G, NB])
        mask2 = sb("mask2", [P, NB, G])
        ln_neg_mean = sb("ln_neg_mean", [P, NB])
        share = (obuf, x1_buf)
        centred_sq = [ring[:, i, :] for i in range(2)]
        ln_var = sb("ln_var", [P, NB])
        ln_scale = sb("ln_scale", [P, NB])
        ln_bias = sb("ln_bias", [P, NB])
        squares = sb("squares", [P, NB])
        norm = sb("norm", [P, NB])
        acc = [ctx.enter_context(nc.psum_tensor(f"acc2{i}", [P, 512], F32)) for i in range(NQ)]
        pe_a = [ctx.enter_context(nc.psum_tensor(f"pe_a{i}", [P, 512], F32)) for i in range(2)]
        pe_x = [ctx.enter_context(nc.psum_tensor(f"pe_x{i}", [P, 512], F32)) for i in range(2)]
        bias_row = [w[:, i, :] for i in (2, 5, 8)]
        gains = [w[:, i, :] for i in (9, 15, 17)]
        shifts = [w[:, i, :] for i in (10, 16, 18)]
        bl = w[:, 11, :]

        consts = sem("c_consts")
        params_in = sem("c_params_in")
        h_in = [sem(f"h_in{i}") for i in range(2)]
        tile_in = [sem(f"c_tile_in{i}") for i in range(RING)]
        keep_in = [sem(f"keep_in{i}") for i in range(KRING // 2)]
        masked = sem("masked")
        deg_added_pool = sem("deg_added_pool")
        deg_added_dve = sem("deg_added_dve")
        deg_done = sem("deg_done")
        deg_read = sem("deg_read")
        step = sem("c_step")
        pool_step = sem("c_pool_step")
        act_step = sem("c_act_step")
        summed = sem("summed")
        bn_var = sem("bn_var")
        bn_root = sem("bn_root")
        bn_ready = sem("bn_ready")
        bn_turned = sem("bn_turned")
        bn_cols = sem("bn_cols")
        ln_mean_ready = sem("ln_mean_ready")
        ln_squared = sem("ln_squared")
        ln_var_ready = sem("ln_var_ready")
        ln_root = sem("ln_root")
        ln_scale_ready = sem("ln_scale_ready")
        ln_done = sem("ln_done")
        share_taken = sem("share_taken")
        share_added = sem("share_added")
        centred = sem("centred")
        squares_ready = sem("squares_ready")
        squares_added = sem("squares_added")
        x1_stored = [sem(f"x1_stored{i}") for i in range(2)]
        x1_in = sem("x1_in")
        x1_added = sem("x1_added")
        h_ready = sem("h_ready")
        h_turned = sem("h_turned")
        h_t_ready = sem("h_t_ready")
        y_done = sem("y_done")
        y_read = sem("y_read")
        tile_used = sem("c_tile_used")
        agg_ready = sem("c_agg_ready")
        out_done = sem("out_done")
        out_read = sem("out_read")
        out_ready = sem("out_ready")
        norm_root = sem("norm_root")
        norm_ready = sem("norm_ready")
        r_ready = sem("r_ready")
        r_squared = sem("r_squared")
        r_summed = sem("r_summed")
        squares_summed = sem("squares_summed")
        r_stored = sem("r_stored")
        out_scaled = sem("out_scaled")
        out_stored = sem("out_stored")
        block = ctx.enter_context(nc.Block())

        def wait(eng, s, value):
            if value > 0:
                eng.wait_ge(s, value)

        def deg_count(t, by_dve):
            return sum((i % NB in DVE_DEG) == by_dve for i in range(min(t, G * NB)))

        def tile(t):
            return ring[:, t % RING, :]

        def r_squares(n):
            return x1_buf[:].rearrange("p a c -> p (a c)") if n < 2 * G else agg_t[:]

        @block.sync
        def _(sp):
            sp.dma_start(w[:], params[:, 1:20, :]).then_inc(params_in, 16)

            for n in range(LAST):
                g = n % G
                for j in range(NB):
                    t = n * NB + j
                    rows = slice(j * P, (j + 1) * P)
                    wait(sp, tile_used, t - RING + 1)
                    wait(sp, deg_added_pool, deg_count(t - RING + 1, False))
                    wait(sp, deg_added_dve, deg_count(t - RING + 1, True))
                    sp.dma_start(tile(t), adj_t[g, rows, :]).then_inc(tile_in[t % RING], 16)
                    if j % 2 == 0:
                        wait(sp, masked, t - KRING + 2)
                        sp.dma_start(keep[:, t % KRING:t % KRING + 2, :],
                                     keep_dram[g, j * P:(j + 2) * P, :].rearrange("(a p) c -> p a c", p=P)
                                     ).then_inc(keep_in[t // 2 % (KRING // 2)], 16)
                    if j == 5 and n >= 2 * G:
                        wait(sp, x1_added, g)
                        if g == 0:
                            sp.wait_ge(r_summed, 2 * 2 * G * NQ)
                            sp.wait_ge(squares_summed, 2 * NQ)
                            for i in range(2):
                                sp.wait_ge(x1_stored[i], 16 * G // 2)
                        sp.dma_start(x1_buf[:], x1_dram[g]).then_inc(x1_in, 16)

        @block.gpsimd
        def _(pool):
            nc.gpsimd.memset(ident[:], 0.0).then_inc(consts, 1)
            nc.gpsimd.memset(ones[:], 1.0).then_inc(consts, 1)
            pool.wait_ge(consts, 2)
            nc.gpsimd.affine_select(out=ident[:], in_=ident[:], compare_op=ALU.not_equal, fill=1.0, base=0,
                                    pattern=[[-1, P]], channel_multiplier=1).then_inc(consts, 1)
            steps = [0]

            def then(ins):
                steps[0] += 1
                ins.then_inc(pool_step, 1)
                pool.wait_ge(pool_step, steps[0])

            def add_sums(n, q):
                if q == 0:
                    pool.wait_ge(r_ready, (n + 1) * NB)
                    if n % G < G - 1:
                        pool.wait_ge(r_squared, n + 1)
                cols = slice(512 * q, 512 * q + 512)
                r = obuf[:, 4 * q:4 * q + 4, :].rearrange("p a c -> p (a c)")
                if n % G == G - 1:
                    nc.gpsimd.tensor_tensor(sums[:, 0, :], sums[:, 0, :], r, ALU.add).then_inc(r_summed, 2)
                    pool.wait_ge(r_summed, 2 * (n * NQ + q + 1))
                    return
                nc.gpsimd.tensor_tensor(sums[:, 0, :], sums[:, 0, :], r, ALU.add).then_inc(r_summed, 1)
                nc.gpsimd.tensor_tensor(sums[:, 1, :], sums[:, 1, :], r_squares(n)[:, cols], ALU.add).then_inc(r_summed, 1)
                pool.wait_ge(r_summed, 2 * (n * NQ + q + 1))

            for n in range(LAST):
                p, g = divmod(n, G)
                if g == 0:
                    wait(pool, summed, p)
                    then(nc.gpsimd.memset(sums[:], 0.0))
                for j in range(NB):
                    t = n * NB + j
                    if p == 0 and j not in DVE_DEG:
                        pool.wait_ge(masked, t + 1)
                        if j == 0:
                            wait(pool, deg_done, n - 1)
                            nc.gpsimd.tensor_copy(deg_pool[n % 2], tile(t)).then_inc(deg_added_pool, 1)
                        else:
                            pool.wait_ge(deg_added_pool, deg_count(t, False))
                            nc.gpsimd.tensor_tensor(deg_pool[n % 2], deg_pool[n % 2], tile(t), ALU.add).then_inc(deg_added_pool, 1)
                    if g > 0 and 10 <= j < 10 + NQ:
                        add_sums(n - 1, j - 10)
                if g == G - 1:
                    for q in range(NQ):
                        add_sums(n, q)
            for g in range(G):
                pool.wait_ge(ln_scale_ready, G + g + 1)
                nc.gpsimd.tensor_tensor(y[:, g], y[:, g], over_columns(ln_scale[:], NB), ALU.mult).then_inc(out_scaled, 1)
                pool.wait_ge(out_scaled, g + 1)
                pool.dma_start(out[g], y[:, g]).then_inc(out_stored, 16)
            pool.wait_ge(out_stored, 16 * G)

        @block.scalar
        def _(act):
            steps = [0]

            def load_h(n):
                wait(act, tile_used, min(n - 1, LAST) * NB)
                wait(act, h_turned, (n - 1) * NQ)
                if n >= 2:
                    act.wait_ge(x1_stored[n % 2], 16 * min(n // 2, G // 2))
                if n >= G:
                    act.wait_ge(r_stored, 16 * (n - G + 1))
                src = u_dram if n < G else r_dram
                act.dma_start(hbuf[n % 2][:], src[n % G]).then_inc(h_in[n % 2], 16)

            def turn(n):
                for q in range(NQ):
                    act.wait_ge(h_turned, n * NQ + q + 1)
                    if q == 0 and n >= 2:
                        act.wait_ge(out_done, min(n - 1, LAST) * NQ)
                        wait(act, y_done, (n - 1 - G) * NQ)
                    src = rows4(pe_a[q % 2])
                    dst = h_t[n % 2][:, 4 * q:4 * q + 4, :]
                    if n < LAST:
                        nc.scalar.activation(dst, src, ACT.Copy).then_inc(h_t_ready, 1)
                    else:
                        nc.scalar.activation(dst, src, ACT.Identity, scale=gain_col[:], bias=shift_col[:]).then_inc(h_t_ready, 1)

            def ln_squares(n):
                act.wait_ge(ln_mean_ready, n + 1)
                wait(act, r_summed, 2 * (n - 2) * NQ)
                for i in range(NB):
                    nc.scalar.activation(x1_buf[:, i, :], hbuf[n % 2][:, i, :], ACT.Square, bias=ln_neg_mean[:, i:i + 1],
                                         accum_out=ln_var[:, i:i + 1]).then_inc(ln_squared, 1)
                act.wait_ge(ln_var_ready, n + 1)
                nc.scalar.activation(ln_scale[:], ln_var[:], ACT.Sqrt).then_inc(ln_root, 1)

            def ln_apply(n):
                act.wait_ge(ln_scale_ready, n + 1)
                for i in range(NB):
                    nc.scalar.activation(hbuf[n % 2][:, i, :], hbuf[n % 2][:, i, :], ACT.Identity, scale=ln_scale[:, i:i + 1],
                                         bias=ln_bias[:, i:i + 1]).then_inc(ln_done, 1)
                store_x1(n)

            def store_x1(n):
                act.wait_ge(ln_done, (n + 1) * NB)
                act.dma_start(x1_dram[n], hbuf[n % 2][:]).then_inc(x1_stored[n % 2], 16)

            def norm_squares(n):
                act.wait_ge(out_ready, n + 1)
                act.wait_ge(out_done, (n + 1) * NQ)
                for i in range(NB):
                    nc.scalar.activation(agg_t[:, i * P:(i + 1) * P], obuf[:, i, :], ACT.Square,
                                         accum_out=squares[:, i:i + 1]).then_inc(act_step, 1)
                steps[0] += NB
                act.wait_ge(act_step, steps[0])
                nc.scalar.activation(norm[:], squares[:], ACT.Sqrt).then_inc(norm_root, 1)

            def norm_apply(n):
                act.wait_ge(norm_ready, n + 1)
                for i in range(NB):
                    nc.scalar.activation(obuf[:, i, :], obuf[:, i, :], ACT.Relu, scale=norm[:, i:i + 1]).then_inc(r_ready, 1)
                act.wait_ge(r_ready, (n + 1) * NB)
                act.dma_start(r_dram[n % G], obuf[:]).then_inc(r_stored, 16)
                nc.scalar.activation(r_squares(n), obuf[:].rearrange("p a c -> p (a c)"), ACT.Square).then_inc(r_squared, 1)

            def bn(p):
                act.wait_ge(bn_var, p)
                nc.scalar.activation(var[:], var[:], ACT.Sqrt).then_inc(bn_root, 1)

            load_h(0)
            load_h(1)
            ln_squares(0)
            ln_apply(0)
            turn(0)
            for n in range(LAST):
                p, g = divmod(n, G)
                if g == 0 and p > 0:
                    bn(p)
                    turn(n)
                if p == 0 and g + 1 < G:
                    ln_squares(n + 1)
                if g > 0:
                    norm_squares(n - 1)
                if g > 0:
                    norm_apply(n - 1)
                if p == 0 and g + 1 < G:
                    ln_apply(n + 1)
                act.wait_ge(tile_used, (n + 1) * NB)
                if n > 2 * G:
                    act.wait_ge(r_summed, 2 * n * NQ)
                for q in range(NQ):
                    nc.scalar.activation(agg_t[:, 512 * q:512 * q + 512], acc[q][:], ACT.Copy).then_inc(agg_ready, 1)
                load_h(n + 2)
                if g + 1 < G:
                    turn(n + 1)
                if g == G - 1:
                    norm_squares(n)
                    norm_apply(n)
            bn(PASSES)
            act.wait_ge(bn_cols, 1)

            def take_share(g):
                if g == 0:
                    act.wait_ge(x1_added, G)
                    act.wait_ge(r_stored, 16 * LAST)
                    act.wait_ge(r_summed, 2 * LAST * NQ)
                if g >= 2:
                    act.wait_ge(share_added, g - 1)
                for i in range(NB):
                    q, a = divmod(i, 4)
                    if a == 0:
                        act.wait_ge(y_done, (2 * G + g) * NQ + q + 1)
                    nc.scalar.activation(share[g % 2][:, i, :], pe_x[q % 2][:, a * P:(a + 1) * P], ACT.Copy,
                                         scale=mask2[:, i, g:g + 1]).then_inc(share_taken, 1)

            def root(g):
                act.wait_ge(ln_var_ready, G + g + 1)
                nc.scalar.activation(ln_scale[:], ln_var[:], ACT.Sqrt).then_inc(ln_root, 1)

            turn(LAST)
            take_share(0)
            load_h(LAST + 2)
            turn(LAST + 1)
            for g in range(G):
                if g + 1 < G:
                    take_share(g + 1)
                if g + 3 < G:
                    load_h(LAST + g + 3)
                if g + 2 < G:
                    turn(LAST + g + 2)
                act.wait_ge(centred, g + 1)
                wait(act, squares_added, g - 1)
                nc.scalar.activation(centred_sq[g % 2], y[:, g].rearrange("p a c -> p (a c)"), ACT.Square).then_inc(squares_ready, 1)
                if g > 0:
                    root(g - 1)
            root(G - 1)
            for i in range(2):
                act.wait_ge(x1_stored[i], 16 * G // 2)

        @block.tensor
        def _(pe):
            pe.wait_ge(consts, 3)
            pe.wait_ge(params_in, 16)

            def batch_sums(p):
                pe.wait_ge(r_summed, 2 * p * G * NQ)
                pe.wait_ge(squares_summed, p * NQ)
                pe.wait_ge(out_read, p * G * NQ)
                for i in range(2):
                    for a in range(4):
                        mm = pe.matmul(pe_x[0][:, i * P:(i + 1) * P], ones[:], sums[:, i, a * P:(a + 1) * P],
                                       start=(a == 0), stop=(a == 3))
                mm.then_inc(summed, 1)

            def turn_h(n):
                if n < G:
                    pe.wait_ge(ln_done, (n + 1) * NB)
                elif n < LAST:
                    pe.wait_ge(h_ready, n - G + 1)
                else:
                    pe.wait_ge(h_in[n % 2], 16 * (n // 2 + 1))
                for q in range(NQ):
                    wait(pe, h_t_ready, n * NQ + q - 1)
                    wait(pe, out_read, min(n if n % G == 0 else n - 1, LAST) * NQ)
                    for a in range(4):
                        mm = pe.transpose(pe_a[q % 2][:, a * P:(a + 1) * P], hbuf[n % 2][:, 4 * q + a, :], ident[:])
                    mm.then_inc(h_turned, 1)

            def wl_share(n):
                wl = w[:, 12 + n // G - 1, :]
                m = n - G
                for q in range(NQ):
                    pe.wait_ge(h_t_ready, n * NQ + q + 1)
                    wait(pe, y_read, min(m * NQ + q - 1, 2 * G * NQ))
                    if n >= LAST:
                        wait(pe, share_taken, 4 * ((n - LAST) * NQ + q - 1))
                    for a in range(4):
                        mm = pe.matmul(pe_x[q % 2][:, a * P:(a + 1) * P], h_t[n % 2][:, 4 * q + a, :], wl, start=True, stop=True)
                    mm.then_inc(y_done, 1)

            def degrees(n):
                pe.wait_ge(deg_added_pool, deg_count((n + 1) * NB, False))
                pe.wait_ge(deg_added_dve, deg_count((n + 1) * NB, True))
                wait(pe, out_read, n * NQ)
                pe.wait_ge(h_t_ready, min(n + 2, G) * NQ)
                for i in range(NB):
                    cols = slice(i * P, (i + 1) * P)
                    pe.matmul(pe_x[0][:, i:i + 1], deg_pool[n % 2][:, cols], ones[:, 0:1], start=True, stop=False)
                    mm = pe.matmul(pe_x[0][:, i:i + 1], deg_dve[n % 2][:, cols], ones[:, 0:1], start=False, stop=True)
                mm.then_inc(deg_done, 1)
                pe.wait_ge(deg_read, n + 1)

            def output(n, ahead):
                p = n // G
                wr, wx = w[:, 3 * p, :], w[:, 3 * p + 1, :]
                if p == 0:
                    degrees(n)
                pe.wait_ge(h_t_ready, ahead * NQ)
                wait(pe, y_read, (ahead - G) * NQ)
                for q in range(NQ):
                    pe.wait_ge(agg_ready, n * NQ + q + 1)
                    wait(pe, out_read, n * NQ + q - 1)
                    for a in range(4):
                        i = 4 * q + a
                        cols = slice(a * P, (a + 1) * P)
                        pe.matmul(pe_a[q % 2][:, cols], agg_t[:, i * P:(i + 1) * P], wr, start=True, stop=True)
                        mm = pe.matmul(pe_x[q % 2][:, cols], h_t[n % 2][:, i, :], wx, start=True, stop=True)
                    mm.then_inc(out_done, 1)

            turn_h(0)
            for n in range(LAST):
                p, g = divmod(n, G)
                if g == 0 and p > 0:
                    batch_sums(p)
                    turn_h(n)
                    wl_share(n)
                wait(pe, agg_ready, n * NQ)
                for j in range(NB):
                    t = n * NB + j
                    if j == DELAY and g > 0 and p == 0:
                        output(n - 1, n + 1)
                    pe.wait_ge(masked, t + 1)
                    for q in range(NQ):
                        mm = pe.matmul(acc[q][:], hbuf[n % 2][:, j, :], ring[:, t % RING, 512 * q:512 * q + 512],
                                       start=(j == 0), stop=(j == NB - 1))
                    mm.then_inc(tile_used, 1)
                if g + 1 < G:
                    turn_h(n + 1)
                    if p > 0:
                        wl_share(n + 1)
                if g == G - 1:
                    output(n, n + 1)
                elif p > 0:
                    output(n, n + 2)
            batch_sums(PASSES)
            pe.wait_ge(bn_ready, PASSES)
            pe.transpose(pe_x[1][:, 0:P], gain[:], ident[:])
            pe.transpose(pe_x[1][:, P:2 * P], shift[:], ident[:]).then_inc(bn_turned, 1)
            pe.wait_ge(bn_cols, 1)
            turn_h(LAST)
            for g in range(G):
                wl_share(LAST + g)
                if g + 1 < G:
                    turn_h(LAST + g + 1)

        @block.vector
        def _(dve):
            v = nc.vector
            steps = [0]

            def then(ins):
                steps[0] += 1
                ins.then_inc(step, 1)
                dve.wait_ge(step, steps[0])

            done = [0]

            def mask_until(t_end):
                for t in range(done[0], min(t_end, LAST * NB)):
                    done[0] += 1
                    dve.wait_ge(keep_in[t // 2 % (KRING // 2)], 16 * (t // KRING + 1))
                    dve.wait_ge(tile_in[t % RING], 16 * (t // RING + 1))
                    v.scalar_tensor_tensor(tile(t), tile(t), 0.0, keep[:, t % KRING, :], ALU.max, ALU.mult).then_inc(masked, 1)
                    if t < G * NB and t % NB in DVE_DEG:
                        dve.wait_ge(masked, t + 1)
                        if t % NB == DVE_DEG[0]:
                            wait(dve, deg_done, t // NB - 1)
                            v.tensor_copy(deg_dve[t // NB % 2], tile(t)).then_inc(deg_added_dve, 1)
                        else:
                            dve.wait_ge(deg_added_dve, deg_count(t, True))
                            v.tensor_tensor(deg_dve[t // NB % 2], deg_dve[t // NB % 2], tile(t), ALU.add).then_inc(deg_added_dve, 1)

            def ln_mean(k):
                if k < G:
                    dve.wait_ge(h_in[k % 2], 16 * (k // 2 + 1))
                    src = hbuf[k % 2][:]
                else:
                    src = y[:, k - G]
                wait(dve, ln_done, min(k, G) * NB)
                then(v.tensor_reduce(ln_neg_mean[:], src, AX.X, ALU.add))
                v.tensor_scalar(ln_neg_mean[:], ln_neg_mean[:], -1.0 / P, None, ALU.mult).then_inc(ln_mean_ready, 1)

            def ln_variance(k):
                if k < G:
                    dve.wait_ge(ln_squared, (k + 1) * NB)
                v.tensor_scalar(ln_var[:], ln_var[:], 1.0 / P, 1e-5, ALU.mult, ALU.add).then_inc(ln_var_ready, 1)

            def ln_scales(k):
                dve.wait_ge(ln_root, k + 1)
                if k >= G:
                    v.reciprocal(ln_scale[:], ln_scale[:]).then_inc(ln_scale_ready, 1)
                    return
                then(v.reciprocal(ln_scale[:], ln_scale[:]))
                v.tensor_tensor(ln_bias[:], ln_neg_mean[:], ln_scale[:], ALU.mult).then_inc(ln_scale_ready, 1)

            def batch_norm(p):
                M = 1.0 / (G * N)
                dve.wait_ge(summed, p)
                then(v.tensor_scalar(mean[:], pe_x[0][:, 0:P], M, None, ALU.mult))
                then(v.tensor_tensor(gain[:], mean[:], mean[:], ALU.mult))
                then(v.scalar_tensor_tensor(var[:], pe_x[0][:, P:2 * P], M, gain[:], ALU.mult, ALU.subtract))
                then(v.tensor_scalar(var[:], var[:], 0.0, None, ALU.max))
                v.tensor_scalar(var[:], var[:], 1e-5, None, ALU.add).then_inc(bn_var, 1)
                dve.wait_ge(bn_root, p)
                then(v.reciprocal(gain[:], var[:]))
                then(v.tensor_tensor(gain[:], gain[:], gains[p - 1], ALU.mult))
                then(v.tensor_tensor(shift[:], mean[:], gain[:], ALU.mult))
                v.tensor_tensor(shift[:], shifts[p - 1], shift[:], ALU.subtract).then_inc(bn_ready, 1)
                dve.wait_ge(bn_ready, p)

            def normalize(n):
                dve.wait_ge(h_in[n % 2], 16 * (n // 2 + 1))
                h = hbuf[n % 2]
                then(v.tensor_tensor(h[:], h[:], over_blocks(gain[:], NB), ALU.mult))
                v.tensor_tensor(h[:], h[:], over_blocks(shift[:], NB), ALU.add).then_inc(h_ready, 1)

            def add_y(n):
                p, g = divmod(n, G)
                m = n - G
                for q in range(NQ):
                    dve.wait_ge(y_done, m * NQ + q + 1)
                    yq = y[:, g, 4 * q:4 * q + 4, :]
                    if p == 1:
                        v.tensor_copy(yq, rows4(pe_x[q % 2])).then_inc(y_read, 1)
                    else:
                        v.tensor_tensor(yq, yq, rows4(pe_x[q % 2]), ALU.add).then_inc(y_read, 1)

            def add_x1(n):
                g = n % G
                yg = y[:, g]
                dve.wait_ge(y_read, (n - G + 1) * NQ)
                then(v.tensor_tensor(yg, yg, over_columns(maskv[:, :, g], NB), ALU.mult))
                then(v.tensor_tensor(yg, yg, over_blocks(bl, NB), ALU.add))
                then(v.tensor_tensor(yg, yg, over_columns(maskv[:, :, g], NB), ALU.mult))
                dve.wait_ge(x1_in, 16 * (g + 1))
                v.tensor_tensor(yg, yg, x1_buf[:], ALU.add).then_inc(x1_added, 1)

            def read_out(n):
                g = n % G
                wait(dve, r_stored, 16 * n)
                wait(dve, r_summed, 2 * n * NQ)
                wait(dve, r_squared, n)
                for q in range(NQ):
                    dve.wait_ge(out_done, n * NQ + q + 1)
                    o = obuf[:, 4 * q:4 * q + 4, :]
                    then(v.tensor_tensor(o, rows4(pe_a[q % 2]), over_columns(deg_inv[:, g, 4 * q:4 * q + 4], 4), ALU.mult))
                    v.tensor_tensor(o, o, rows4(pe_x[q % 2]), ALU.add).then_inc(out_read, 1)
                dve.wait_ge(out_read, (n + 1) * NQ)
                v.tensor_tensor(obuf[:], obuf[:], over_blocks(bias_row[n // G], NB), ALU.add).then_inc(out_ready, 1)

            def norm_scale(n):
                dve.wait_ge(norm_root, n + 1)
                then(v.tensor_scalar(norm[:], norm[:], 1e-12, None, ALU.max))
                then(v.reciprocal(norm[:], norm[:]))
                v.tensor_tensor(norm[:], norm[:], maskv[:, :, n % G], ALU.mult).then_inc(norm_ready, 1)

            def degree(n):
                dve.wait_ge(deg_done, n + 1)
                v.tensor_scalar(deg_inv[:, n, :], pe_x[0][:, 0:NB], 1.0, None, ALU.max).then_inc(deg_read, 1)
                dve.wait_ge(deg_read, n + 1)
                then(v.reciprocal(deg_inv[:, n, :], deg_inv[:, n, :]))

            dve.wait_ge(params_in, 16)
            then(v.tensor_tensor(mask2[:], maskv[:], maskv[:], ALU.mult))
            ln_mean(0)
            mask_until(1)
            ln_variance(0)
            mask_until(2)
            ln_scales(0)
            for n in range(LAST):
                p, g = divmod(n, G)
                first = n * NB
                if g == 0 and p > 0:
                    batch_norm(p)
                    normalize(n)
                    add_y(n)
                if p == 0:
                    if g + 1 < G:
                        ln_mean(n + 1)
                    mask_until(first + DELAY + 2)
                    if g > 0:
                        degree(n - 1)
                        read_out(n - 1)
                    if g + 1 < G:
                        ln_variance(n + 1)
                        mask_until(first + 8)
                        ln_scales(n + 1)
                    mask_until(first + 9)
                    if g > 0:
                        norm_scale(n - 1)
                else:
                    mask_until(first + 5)
                    if g > 0:
                        norm_scale(n - 1)
                    mask_until(first + 7)
                    if g + 1 < G:
                        normalize(n + 1)
                mask_until(first + 12)
                if p == PASSES - 1:
                    add_x1(n)
                mask_until(first + NB + 2)
                if g + 1 < G and p > 0:
                    add_y(n + 1)
                if g == G - 1 or p > 0:
                    if p == 0:
                        degree(n)
                    read_out(n)
                if g == G - 1:
                    norm_scale(n)
                    dve.wait_ge(r_squared, n + 1)
                    for q in range(NQ):
                        v.tensor_tensor(sums[:, 1, :], sums[:, 1, :], r_squares(n)[:, 512 * q:512 * q + 512],
                                        ALU.add).then_inc(squares_summed, 1)
                        dve.wait_ge(squares_summed, p * NQ + q + 1)
            batch_norm(PASSES)
            dve.wait_ge(bn_turned, 1)
            then(v.tensor_copy(gain_col[:], pe_x[1][:, 0:1]))
            v.tensor_copy(shift_col[:], pe_x[1][:, P:P + 1]).then_inc(bn_cols, 1)
            for g in range(G + 1):
                if g < G:
                    yg = y[:, g]
                    dve.wait_ge(share_taken, NB * (g + 1))
                    v.tensor_tensor(yg, yg, share[g % 2][:], ALU.add).then_inc(share_added, 1)
                    dve.wait_ge(share_added, g + 1)
                if g >= 2:
                    ln_scales(G + g - 2)
                if g < G:
                    ln_mean(G + g)
                    dve.wait_ge(ln_mean_ready, G + g + 1)
                    v.tensor_tensor(yg, yg, over_columns(ln_neg_mean[:], NB), ALU.add).then_inc(centred, 1)
                if g >= 1:
                    dve.wait_ge(squares_ready, g)
                    wait(dve, ln_scale_ready, G + g - 1)
                    v.tensor_reduce(ln_var[:], centred_sq[(g - 1) % 2].rearrange("p (a c) -> p a c", c=P), AX.X,
                                    ALU.add).then_inc(squares_added, 1)
                    dve.wait_ge(squares_added, g)
                    wait(dve, out_scaled, g - 1)
                    ln_variance(G + g - 1)
            ln_scales(2 * G - 1)


def program(nc, adj, adj_t, mask, x, x_diag, params, out):
    G, N, _ = adj.shape
    NB = N // P

    def scratch(name, shape, dt):
        return nc.dram_tensor(name, shape, dt).ap()

    keep_dram = scratch("keep_dram", (G, N, N), U8)
    removed_cols = scratch("removed_cols", (G, N, N), U8)
    u_dram = scratch("u_dram", (G, P, NB, P), F32)
    x1_dram = scratch("x1_dram", (G, P, NB, P), F32)
    r_dram = scratch("r_dram", (G, P, NB, P), F32)
    with ExitStack() as ctx:
        maskv = ctx.enter_context(nc.sbuf_tensor("maskv", [P, NB, G], F32))
        dilate(nc, adj, adj_t, mask, x, x_diag, params, keep_dram, removed_cols, u_dram, maskv)
        passes(nc, adj_t, params, keep_dram, u_dram, maskv, x1_dram, r_dram, out)


def kernel(**inputs):
    import numpy as _np
    import concourse.bacc as _bacc
    from concourse import mybir as _mybir
    from concourse.bass_utils import run_bass_kernel_spmd as _run

    adj, x, mask = (_np.asarray(inputs[n]) for n in ("adj", "x", "nodemask"))
    G, N, D = x.shape
    NB = N // P

    def weight(name):
        return _np.asarray(inputs[name]).reshape(-1, P, D)

    def spread(name):
        return _np.broadcast_to(_np.asarray(inputs["L1_gnn_" + name]), (1, P, D))

    params = _np.concatenate(
        [weight("L0_gnn_kernel"), weight("L1_gnn_Wr1"), weight("L1_gnn_Wx1"), spread("b1"),
         weight("L1_gnn_Wr2"), weight("L1_gnn_Wx2"), spread("b2"), weight("L1_gnn_Wr3"), weight("L1_gnn_Wx3"),
         spread("b3"), spread("g1"), spread("be1"), spread("bl"), weight("L1_gnn_Wl"),
         spread("g2"), spread("be2"), spread("g3"), spread("be3")]).transpose(1, 0, 2)
    laid_out = {
        "adj": adj,
        "adj_t": adj.transpose(0, 2, 1),
        "mask": mask.reshape(G, NB, P).transpose(2, 1, 0),
        "x": x.reshape(G, NB, P, D).transpose(0, 2, 1, 3),
        "x_diag": _np.diagonal(adj, axis1=1, axis2=2).reshape(G, NB, P).transpose(2, 0, 1),
        "params": params,
    }
    nc = _bacc.Bacc("TRN2", target_bir_lowering=False, num_devices=1)
    arrays, args = {}, []
    for name, a in laid_out.items():
        a = _np.ascontiguousarray(a)
        arrays[f"in_{name}_dram"] = a
        args.append(nc.dram_tensor(f"in_{name}_dram", a.shape, _mybir.dt.from_np(a.dtype), kind="ExternalInput").ap())
    args.append(nc.dram_tensor("out_dram", (G, P, NB, D), F32, kind="ExternalOutput").ap())
    program(nc, *args)
    r = _run(nc, [arrays], core_ids=[0])
    return r.results[0]["out_dram"].transpose(0, 2, 1, 3).reshape(G, N, D)
```
